# Optimizing a Trainium2 kernel written in Bass

```python
import numpy as np
import jax
import jax.numpy as jnp

def _softmax(x, axis=-1):
    return jax.nn.softmax(x, axis=axis)

def _gelu(x):
    return jax.nn.gelu(x, approximate=True)

def _silu(x):
    return jax.nn.silu(x)

def _sigmoid(x):
    return jax.nn.sigmoid(x)

def _layernorm(x, axis=-1, eps=1e-05):
    m = jnp.mean(x, axis=axis, keepdims=True)
    v = jnp.var(x, axis=axis, keepdims=True)
    return (x - m) / jnp.sqrt(v + eps)

def _scatter_add(tgt, idx, src, axis=0):
    return tgt.at[idx].add(src)

def _segment_sum(src, seg, n):
    return jax.ops.segment_sum(src, seg, n)
kernel_name = 'mk_xattn_ffn_d2_seqx_r8_cf6c20'

def setup_inputs(seed: int=0):
    np.random.seed(seed)
    _w = jnp.asarray

    def _rec_inputs():
        import jax
        import jax.numpy as jnp
        _rk = jax.random.key(seed)
        x = -0.0002928 + 1 * jax.random.normal(jax.random.fold_in(_rk, 1), (2, 512, 128), jnp.float32)
        _lenS = 512 - jax.random.randint(jax.random.fold_in(_rk, 7), (2,), 0, max(1, 512 // 4) + 1, jnp.int32)
        _lenS2 = 77 - jax.random.randint(jax.random.fold_in(_rk, 8), (2,), 0, max(1, 77 // 4) + 1, jnp.int32)
        _ctx_1024P = jax.random.normal(jax.random.fold_in(_rk, 11), (2, 16, 128), jnp.float32)
        _ctx_1024c = jax.random.dirichlet(jax.random.fold_in(_rk, 511), 0.3 * jnp.ones((16,), jnp.float32), (2, 77))
        _ctx_1024t = jnp.einsum('bsk,bkd->bsd', _ctx_1024c, _ctx_1024P)
        _ctx_1024t = _ctx_1024t * jax.lax.rsqrt(jnp.mean(jnp.square(_ctx_1024t)) + 1e-12) * 0.953939
        ctx_1024 = -1.39393e-06 + 0.999914 * (_ctx_1024t + 0.3 * jax.random.normal(jax.random.fold_in(_rk, 611), (2, 77, 128), jnp.float32))
        return (x, ctx_1024)
    x, ctx_1024 = _rec_inputs()

    def _L0_xattn_setup():
        import jax, jax.numpy as jnp
        import numpy as np
        D_MODEL = 128
        NUM_HEADS = 16
        HEAD_DIM = D_MODEL // NUM_HEADS
        SCALE = HEAD_DIM ** (-0.5)
        BIAS_LEN = 128
        ROPE_BASE = 10000.0
        LN_EPS = 1e-05

        def _layernorm(x, gamma, beta):
            mu = jnp.mean(x, axis=-1, keepdims=True)
            var = jnp.mean(jnp.square(x - mu), axis=-1, keepdims=True)
            return (x - mu) * jax.lax.rsqrt(var + LN_EPS) * gamma + beta

        def _rope(x, cos, sin):
            half = HEAD_DIM // 2
            c = cos[None, None, :, :]
            s = sin[None, None, :, :]
            x_even, x_odd = (x[..., :half], x[..., half:])
            return jnp.concatenate([x_even * c - x_odd * s, x_even * s + x_odd * c], axis=-1)

        def _temporal_bias(L_q, L_kv):
            pos = jnp.arange(BIAS_LEN, dtype=jnp.float32)
            dist = jnp.abs(pos[None, :] - pos[:, None])
            bias = jnp.exp(-dist * 0.1) - dist * 0.05
            if L_q <= BIAS_LEN and L_kv <= BIAS_LEN:
                return bias[:L_q, :L_kv]
            return jax.image.resize(bias, (L_q, L_kv), method='bilinear')
        key = jax.random.key(seed)
        ks = jax.random.split(key, 8)
        B, Lq, Lkv = (8, 64, 64)
        return {'decoder_hidden': jax.random.normal(ks[0], (B, Lq, D_MODEL), jnp.float32), 'encoder_output': jax.random.normal(ks[1], (B, Lkv, D_MODEL), jnp.float32), 'Wqkv': jax.random.normal(ks[2], (3 * D_MODEL, D_MODEL), jnp.float32) * 0.02, 'Wout': jax.random.normal(ks[3], (D_MODEL, D_MODEL), jnp.float32) * 0.02, 'b_out': jnp.zeros((D_MODEL,), jnp.float32), 'Wgate': jax.random.normal(ks[4], (D_MODEL, D_MODEL), jnp.float32) * 0.02, 'b_gate': jnp.zeros((D_MODEL,), jnp.float32), 'gamma': jnp.ones((D_MODEL,), jnp.float32), 'beta': jnp.zeros((D_MODEL,), jnp.float32)}
    _L0_xattn_all = _L0_xattn_setup()
    _L0_xattn_in = {k: v for k, v in _L0_xattn_all.items() if k in ('Wqkv', 'Wout', 'b_out', 'Wgate', 'b_gate', 'gamma', 'beta')}
    del _L0_xattn_all

    def _L0_ffn_setup():
        import jax, jax.numpy as jnp
        import numpy as np
        TOP_K = 2
        TEMP = 1.0
        key = jax.random.key(seed)
        ks = jax.random.split(key, 5)
        B, S, D, E = (4, 256, 128, 8)
        F = 4 * D
        x = jax.random.normal(ks[0], (B, S, D), dtype=jnp.float32)
        Wg = jax.random.normal(ks[1], (D, E), dtype=jnp.float32) * (1.0 / np.sqrt(D))
        bg = jnp.zeros((E,), dtype=jnp.float32)
        W1 = jax.random.normal(ks[2], (E, D, F), dtype=jnp.float32) * (1.0 / np.sqrt(D))
        b1 = jnp.zeros((E, F), dtype=jnp.float32)
        W2 = jax.random.normal(ks[3], (E, F, D), dtype=jnp.float32) * (1.0 / np.sqrt(F))
        b2 = jnp.zeros((E, D), dtype=jnp.float32)
        return {'x': x, 'Wg': Wg, 'bg': bg, 'W1': W1, 'b1': b1, 'W2': W2, 'b2': b2}
    _L0_ffn_all = _L0_ffn_setup()
    _L0_ffn_in = {k: v for k, v in _L0_ffn_all.items() if k in ('Wg', 'bg', 'W1', 'b1', 'W2', 'b2')}
    del _L0_ffn_all

    def _L1_xattn_setup():
        import jax, jax.numpy as jnp
        import numpy as np
        D_MODEL = 128
        N_HEADS = 16
        D_K = D_MODEL // N_HEADS
        key = jax.random.key(seed)
        ks = jax.random.split(key, 11)
        B, L, S = (2, 256, 256)
        scale = 1.0 / np.sqrt(D_MODEL)
        return {'x_q': jax.random.normal(ks[0], (B, L, D_MODEL), jnp.float32), 'x_k': jax.random.normal(ks[1], (B, S, D_MODEL), jnp.float32), 'x_v': jax.random.normal(ks[2], (B, S, D_MODEL), jnp.float32), 'W_Q': jax.random.normal(ks[3], (D_MODEL, D_MODEL), jnp.float32) * scale, 'b_Q': jax.random.normal(ks[4], (D_MODEL,), jnp.float32) * 0.01, 'W_K': jax.random.normal(ks[5], (D_MODEL, D_MODEL), jnp.float32) * scale, 'b_K': jax.random.normal(ks[6], (D_MODEL,), jnp.float32) * 0.01, 'W_V': jax.random.normal(ks[7], (D_MODEL, D_MODEL), jnp.float32) * scale, 'b_V': jax.random.normal(ks[8], (D_MODEL,), jnp.float32) * 0.01, 'W_O': jax.random.normal(ks[9], (D_MODEL, D_MODEL), jnp.float32) * scale, 'b_O': jax.random.normal(ks[10], (D_MODEL,), jnp.float32) * 0.01}
    _L1_xattn_all = _L1_xattn_setup()
    _L1_xattn_in = {k: v for k, v in _L1_xattn_all.items() if k in ('W_Q', 'b_Q', 'W_K', 'b_K', 'W_V', 'b_V', 'W_O', 'b_O')}
    del _L1_xattn_all

    def _L1_ffn_setup():
        import jax, jax.numpy as jnp
        import numpy as np
        NUM_EXPERTS = 8
        TOP_K = 2
        CAP_RATIO = 1.25
        INIT_STD = 0.02
        key = jax.random.key(seed)
        k1, k2, k3, k4 = jax.random.split(key, 4)
        B, T, H, F = (4, 256, 128, 512)
        x = jax.random.normal(k1, (B, T, H), jnp.float32)
        router_w = jax.random.normal(k2, (NUM_EXPERTS, H), jnp.float32) * INIT_STD
        w1 = jax.random.normal(k3, (NUM_EXPERTS, H, F), jnp.float32) * INIT_STD
        w2 = jax.random.normal(k4, (NUM_EXPERTS, F, H), jnp.float32) * INIT_STD
        return {'x': x, 'router_w': router_w, 'w1': w1, 'w2': w2}
    _L1_ffn_all = _L1_ffn_setup()
    _L1_ffn_in = {k: v for k, v in _L1_ffn_all.items() if k in ('router_w', 'w1', 'w2')}
    del _L1_ffn_all
    return {'x': x, 'ctx_1024': ctx_1024, 'L0_xattn_Wqkv': _L0_xattn_in['Wqkv'], 'L0_xattn_Wout': _L0_xattn_in['Wout'], 'L0_xattn_b_out': _L0_xattn_in['b_out'], 'L0_xattn_Wgate': _L0_xattn_in['Wgate'], 'L0_xattn_b_gate': _L0_xattn_in['b_gate'], 'L0_xattn_gamma': _L0_xattn_in['gamma'], 'L0_xattn_beta': _L0_xattn_in['beta'], 'L0_ffn_Wg': _L0_ffn_in['Wg'], 'L0_ffn_bg': _L0_ffn_in['bg'], 'L0_ffn_W1': _L0_ffn_in['W1'], 'L0_ffn_b1': _L0_ffn_in['b1'], 'L0_ffn_W2': _L0_ffn_in['W2'], 'L0_ffn_b2': _L0_ffn_in['b2'], 'L1_xattn_W_Q': _L1_xattn_in['W_Q'], 'L1_xattn_b_Q': _L1_xattn_in['b_Q'], 'L1_xattn_W_K': _L1_xattn_in['W_K'], 'L1_xattn_b_K': _L1_xattn_in['b_K'], 'L1_xattn_W_V': _L1_xattn_in['W_V'], 'L1_xattn_b_V': _L1_xattn_in['b_V'], 'L1_xattn_W_O': _L1_xattn_in['W_O'], 'L1_xattn_b_O': _L1_xattn_in['b_O'], 'L1_ffn_router_w': _L1_ffn_in['router_w'], 'L1_ffn_w1': _L1_ffn_in['w1'], 'L1_ffn_w2': _L1_ffn_in['w2']}

def reference(x, ctx_1024, L0_xattn_Wqkv, L0_xattn_Wout, L0_xattn_b_out, L0_xattn_Wgate, L0_xattn_b_gate, L0_xattn_gamma, L0_xattn_beta, L0_ffn_Wg, L0_ffn_bg, L0_ffn_W1, L0_ffn_b1, L0_ffn_W2, L0_ffn_b2, L1_xattn_W_Q, L1_xattn_b_Q, L1_xattn_W_K, L1_xattn_b_K, L1_xattn_W_V, L1_xattn_b_V, L1_xattn_W_O, L1_xattn_b_O, L1_ffn_router_w, L1_ffn_w1, L1_ffn_w2):
    import jax
    import jax.numpy as jnp

    def _L0_xattn_ref(decoder_hidden, encoder_output, Wqkv, Wout, b_out, Wgate, b_gate, gamma, beta):
        import jax, jax.numpy as jnp
        import numpy as np
        D_MODEL = 128
        NUM_HEADS = 16
        HEAD_DIM = D_MODEL // NUM_HEADS
        SCALE = HEAD_DIM ** (-0.5)
        BIAS_LEN = 128
        ROPE_BASE = 10000.0
        LN_EPS = 1e-05

        def _layernorm(x, gamma, beta):
            mu = jnp.mean(x, axis=-1, keepdims=True)
            var = jnp.mean(jnp.square(x - mu), axis=-1, keepdims=True)
            return (x - mu) * jax.lax.rsqrt(var + LN_EPS) * gamma + beta

        def _rope(x, cos, sin):
            half = HEAD_DIM // 2
            c = cos[None, None, :, :]
            s = sin[None, None, :, :]
            x_even, x_odd = (x[..., :half], x[..., half:])
            return jnp.concatenate([x_even * c - x_odd * s, x_even * s + x_odd * c], axis=-1)

        def _temporal_bias(L_q, L_kv):
            pos = jnp.arange(BIAS_LEN, dtype=jnp.float32)
            dist = jnp.abs(pos[None, :] - pos[:, None])
            bias = jnp.exp(-dist * 0.1) - dist * 0.05
            if L_q <= BIAS_LEN and L_kv <= BIAS_LEN:
                return bias[:L_q, :L_kv]
            return jax.image.resize(bias, (L_q, L_kv), method='bilinear')
        B, L_q, _ = decoder_hidden.shape
        L_kv = encoder_output.shape[1]
        residual = decoder_hidden
        q_in = _layernorm(decoder_hidden, gamma, beta)
        kv_in = _layernorm(encoder_output, gamma, beta)
        q = q_in @ Wqkv[:D_MODEL].T
        k = kv_in @ Wqkv[D_MODEL:2 * D_MODEL].T
        v = kv_in @ Wqkv[2 * D_MODEL:].T
        q = q.reshape(B, L_q, NUM_HEADS, HEAD_DIM).transpose(0, 2, 1, 3)
        k = k.reshape(B, L_kv, NUM_HEADS, HEAD_DIM).transpose(0, 2, 1, 3)
        v = v.reshape(B, L_kv, NUM_HEADS, HEAD_DIM).transpose(0, 2, 1, 3)
        L = max(L_q, L_kv)
        inv_freq = 1.0 / ROPE_BASE ** (jnp.arange(0, HEAD_DIM, 2, dtype=jnp.float32) / HEAD_DIM)
        freqs = jnp.arange(L, dtype=jnp.float32)[:, None] * inv_freq[None, :]
        cos, sin = (jnp.cos(freqs), jnp.sin(freqs))
        q = _rope(q, cos[:L_q], sin[:L_q])
        k = _rope(k, cos[:L_kv], sin[:L_kv])
        scores = jnp.einsum('bhqd,bhkd->bhqk', q, k) * SCALE
        scores = scores + _temporal_bias(L_q, L_kv)[None, None, :, :]
        attn = jax.nn.softmax(scores, axis=-1)
        attended = jnp.einsum('bhqk,bhkd->bhqd', attn, v)
        attended = attended.transpose(0, 2, 1, 3).reshape(B, L_q, D_MODEL)
        attended = attended @ Wout.T + b_out
        gate = jax.nn.sigmoid(attended @ Wgate.T + b_gate)
        output = gate * attended + (1.0 - gate) * residual
        return output

    def _L0_ffn_ref(x, Wg, bg, W1, b1, W2, b2):
        import jax, jax.numpy as jnp
        import numpy as np
        TOP_K = 2
        TEMP = 1.0
        gates = (jnp.einsum('bsd,de->bse', x, Wg) + bg) / (TEMP + 1e-06)
        weights, indices = jax.lax.top_k(gates, TOP_K)
        weights = jax.nn.softmax(weights, axis=-1)
        h = jax.nn.silu(jnp.einsum('bsd,edf->bsef', x, W1) + b1)
        all_out = jnp.einsum('bsef,efd->bsed', h, W2) + b2
        gathered = jnp.take_along_axis(all_out, indices[..., None], axis=2)
        out = jnp.sum(gathered * weights[..., None], axis=2)
        return out

    def _L1_xattn_ref(x_q, x_k, x_v, W_Q, b_Q, W_K, b_K, W_V, b_V, W_O, b_O):
        import jax, jax.numpy as jnp
        import numpy as np
        D_MODEL = 128
        N_HEADS = 16
        D_K = D_MODEL // N_HEADS
        B, L, _ = x_q.shape
        S = x_k.shape[1]
        H, dk = (N_HEADS, D_K)
        Q = (x_q @ W_Q + b_Q).reshape(B, L, H, dk).transpose(0, 2, 1, 3)
        K = (x_k @ W_K + b_K).reshape(B, S, H, dk).transpose(0, 2, 1, 3)
        V = (x_v @ W_V + b_V).reshape(B, S, H, dk).transpose(0, 2, 1, 3)
        scores = jnp.einsum('bhld,bhsd->bhls', Q, K) / jnp.sqrt(jnp.float32(dk))
        attn = jax.nn.softmax(scores, axis=-1)
        ctx = jnp.einsum('bhls,bhsd->bhld', attn, V)
        ctx = ctx.transpose(0, 2, 1, 3).reshape(B, L, H * dk)
        out = ctx @ W_O + b_O
        return out

    def _L1_ffn_ref(x, router_w, w1, w2):
        import jax, jax.numpy as jnp
        import numpy as np
        NUM_EXPERTS = 8
        TOP_K = 2
        CAP_RATIO = 1.25
        INIT_STD = 0.02
        B, T, H = x.shape
        E, K = (NUM_EXPERTS, TOP_K)
        xf = x.reshape(-1, H)
        N = xf.shape[0]
        P = N * K
        capacity = int(CAP_RATio * N * K / E) + 1 if False else int(CAP_RATIO * N * K / E) + 1
        logits = xf @ router_w.T
        probs = jax.nn.softmax(logits, axis=-1)
        k_probs, k_idx = jax.lax.top_k(probs, K)
        k_probs = k_probs / jnp.sum(k_probs, axis=-1, keepdims=True)
        flat_e = k_idx.reshape(-1)
        onehot = jax.nn.one_hot(flat_e, E, dtype=jnp.int32)
        rank = jnp.take_along_axis(jnp.cumsum(onehot, axis=0) - 1, flat_e[:, None], axis=1)[:, 0]
        keep = rank < capacity
        slot = jnp.minimum(rank, capacity - 1)
        token_id = jnp.arange(P) // K
        dispatched = jnp.where(keep[:, None], xf[token_id], 0.0)
        buf = jnp.zeros((E, capacity, H), x.dtype).at[flat_e, slot].add(dispatched)
        h = jax.nn.silu(jnp.einsum('ech,ehf->ecf', buf, w1))
        out_buf = jnp.einsum('ecf,efh->ech', h, w2)
        pair_out = out_buf[flat_e, slot] * keep[:, None].astype(x.dtype)
        combined = jnp.sum(pair_out.reshape(N, K, H) * k_probs[..., None], axis=1)
        return combined.reshape(B, T, H) + x
    x = x + _L0_xattn_ref(_layernorm(x, axis=-1), ctx_1024, L0_xattn_Wqkv, L0_xattn_Wout, L0_xattn_b_out, L0_xattn_Wgate, L0_xattn_b_gate, L0_xattn_gamma, L0_xattn_beta)
    x = x + _L0_ffn_ref(_layernorm(x, axis=-1), L0_ffn_Wg, L0_ffn_bg, L0_ffn_W1, L0_ffn_b1, L0_ffn_W2, L0_ffn_b2)
    x = x + _L1_xattn_ref(_layernorm(x, axis=-1), ctx_1024, ctx_1024, L1_xattn_W_Q, L1_xattn_b_Q, L1_xattn_W_K, L1_xattn_b_K, L1_xattn_W_V, L1_xattn_b_V, L1_xattn_W_O, L1_xattn_b_O)
    x = x + _L1_ffn_ref(_layernorm(x, axis=-1), L1_ffn_router_w, L1_ffn_w1, L1_ffn_w2)
    return x

_drawn_inputs = setup_inputs


def setup_inputs(seed=0):
    import zlib

    import numpy as np

    out = dict(_drawn_inputs(seed))
    spreads = {'L0_xattn_b_out': (0.0, 0.1),
     'L0_xattn_b_gate': (0.0, 0.1),
     'L0_xattn_gamma': (1.0, 0.6),
     'L0_xattn_beta': (0.0, 0.8),
     'L0_ffn_bg': (0.0, 0.1),
     'L0_ffn_b1': (0.0, 0.285),
     'L0_ffn_b2': (0.0, 0.1)}
    factors = {'L0_xattn_Wqkv': 2.816,
     'L0_xattn_Wout': 3.465,
     'L0_xattn_Wgate': 4.768,
     'L1_xattn_b_Q': 8.0,
     'L1_xattn_b_K': 8.0,
     'L1_xattn_b_V': 8.0,
     'L1_xattn_b_O': 8.0,
     'L1_ffn_router_w': 4.7,
     'L1_ffn_w1': 4.174,
     'L1_ffn_w2': 4.169}
    for name, (base, spread) in spreads.items():
        noise = np.random.default_rng([zlib.crc32(name.encode()), seed]).standard_normal(out[name].shape)
        drawn = base * np.exp(spread * noise) if base else spread * noise
        out[name] = jnp.asarray(drawn.astype(out[name].dtype))
    for name, factor in factors.items():
        out[name] = (out[name] * factor).astype(out[name].dtype)
    return out
```

```python
import numpy as np
import concourse.bass as bass
from concourse import mybir
from contextlib import ExitStack

B, T, D = 2, 512, 128
KV = 77
H, DH = 16, 8
P = 128
TILES = B * T // P
TB = T // P
HALF = H // 2
UNITS = 2 * TILES
UB = 2 * TB
HB = HALF // 2
PAIR = 2 * P
E, K2 = 8, 2
FF = 512
FC = FF // P
SLOT = 384
SC = SLOT // P
NSLOT = E * SLOT
CAP_D = int(1.25 * B * T * K2 / E) + 1
EPS = 1e-5
SCALE = DH ** -0.5
GATE_DIV = float(np.float32(1.0) / np.float32(1.0 + 1e-6))

C_COS, C_SIN, C_BIAS, C_MASK, C_IOTA = 0, T, 2 * T, 2 * T + TB * KV, 2 * T + TB * KV + H
C_END = C_IOTA + E
R_BOUT, R_BGATE, R_BO, R_BV, R_BG, R_B2 = 0, D, 2 * D, 3 * D, 4 * D, 4 * D + E
R_END = R_B2 + E * D
V_GAMMA, V_BETA, V_BOUT, V_BQ, V_BK, V_B1 = 0, 1, 2, 3, 4, 5
V_END = V_B1 + E * FC
W_NAMES = ["q0", "q0p", "k0", "k0p", "v0", "out0", "gate0", "q1", "k1", "v1", "o1"]


def resized_bias():
    n = 128
    pos = np.arange(n, dtype=np.float64)
    dist = np.abs(pos[None, :] - pos[:, None])
    bias = np.exp(-dist * 0.1) - dist * 0.05

    def weights(out):
        inv = n / out
        at = (np.arange(out) + 0.5) * inv - 0.5
        w = np.maximum(0.0, 1.0 - np.abs(at[None, :] - np.arange(n)[:, None]) / max(inv, 1.0))
        return w / w.sum(axis=0, keepdims=True)

    return (weights(T).T @ bias @ weights(KV)).astype(np.float32)


def constants():
    c = np.zeros((P, C_END), np.float32)
    half = DH // 2
    inv_freq = 1.0 / 10000.0 ** (np.arange(0, DH, 2, dtype=np.float32) / np.float32(DH))
    freqs = np.arange(T, dtype=np.float32)[:, None] * inv_freq.astype(np.float32)[None, :]
    lane = np.arange(P) % DH
    angle = freqs[:, lane % half].T.astype(np.float32)
    c[:, C_COS:C_COS + T] = np.cos(angle.astype(np.float64))
    c[:, C_SIN:C_SIN + T] = np.where(lane[:, None] < half, -1.0, 1.0) * np.sin(angle.astype(np.float64))
    bias = resized_bias().reshape(TB, P, KV)
    c[:, C_BIAS:C_BIAS + TB * KV] = bias.transpose(1, 0, 2).reshape(P, TB * KV)
    c[:, C_MASK:C_MASK + H] = SCALE * (np.arange(P)[:, None] // DH == np.arange(H)[None, :])
    c[:, C_IOTA:C_IOTA + E] = np.arange(E)[None, :]
    return c


def two_block_kernel(nc, x, ctx, consts, sq, cols, rows, wg, wr, w1b, w2b, w1d, w2d, out):
    F32, BF16, U32 = mybir.dt.float32, mybir.dt.bfloat16, mybir.dt.uint32
    ALU = mybir.AluOpType
    ACT = mybir.ActivationFunctionType
    AX = mybir.AxisListType

    with ExitStack() as stack:
        def sb(name, shape, dt=F32):
            return stack.enter_context(nc.sbuf_tensor(name, shape, dt))

        def sem(name):
            return stack.enter_context(nc.semaphore(name))

        sent = [nc.dram_tensor(f"sent{m}", (NSLOT, D), F32, kind="Internal").ap() for m in range(2)]
        back = [nc.dram_tensor(f"back{m}", (NSLOT + 1, D), F32, kind="Internal").ap() for m in range(2)]

        cst = sb("cst", [P, C_END])
        sqw = sb("sqw", [P, len(W_NAMES), D])
        col = sb("col", [P, V_END])
        row = sb("row", [P, R_END])
        router = sb("router", [P, 2, E])
        w1 = sb("w1", [P, E, FF])
        w2 = sb("w2", [P, E, FC, D])
        zero = sb("zero", [P, SC, D])
        ident = sb("ident", [P, P])
        tri = sb("tri", [P, P], BF16)
        ones = sb("ones", [P, P], BF16)
        power = sb("power", [P, TILES])
        xres = sb("xres", [P, TILES, D])
        hid = sb("hid", [P, TILES, D])
        base = sb("base", [P, TILES, D])
        norm = sb("norm", [P, TILES, D])
        ctxs = sb("ctxs", [KV, B, D])
        ctxn = sb("ctxn", [KV, B, D])
        stats = sb("stats", [P, TILES, 6])
        mv = sb("mv", [P, TILES, 2])
        vare = sb("vare", [P, TILES])
        rstd = sb("rstd", [P, TILES])
        inT = sb("inT", [P, B, T])
        kinT = sb("kinT", [P, B, KV])
        qT = sb("qT", [P, B, T])
        ropeb = sb("ropeb", [P, T])
        kT = sb("kT", [P, B, KV])
        ropek = sb("ropek", [P, B, KV])
        kbd = sb("kbd", [P, B, H, KV])
        vpad = sb("vpad", [KV, B, H, 32])
        onepad = sb("onepad", [KV, 4, 32])
        shifted = sb("shifted", [P, 2, 2, HB, KV])
        probs = sb("probs", [P, 2, 2, HB, KV])
        peak = sb("peak", [P, 2, 2, HB])
        probT = sb("probT", [KV, 2, H, PAIR])
        attT = sb("attT", [P, B, T])
        rden = sb("rden", [P, T])
        yT = sb("yT", [P, T])
        ytok = sb("ytok", [P, TB, D])
        ztok = sb("ztok", [P, TB, D])
        logit = sb("logit", [P, TILES, E])
        top = sb("top", [P, TILES, 8])
        topi = sb("topi", [P, TILES, 8], U32)
        topf = sb("topf", [P, TILES, K2])
        pick = sb("pick", [P, TILES, K2, E])
        picked = sb("picked", [P, TILES, E], BF16)
        ranked = sb("ranked", [P, TILES, K2, E])
        rank = sb("rank", [P, TILES, K2])
        slot = sb("slot", [P, TILES, K2])
        over = sb("over", [P, TILES, K2])
        slotu = sb("slotu", [P, TILES, K2], U32)
        wdif = sb("wdif", [P, TILES])
        wexp = sb("wexp", [P, TILES])
        wden = sb("wden", [P, TILES])
        wtok = sb("wtok", [P, TILES, K2])
        xe = sb("xe", [P, E, SC, D])
        xeT = sb("xeT", [P, 2, SLOT])
        hT = sb("hT", [P, 2, FC, SLOT])
        ye = sb("ye", [P, E, SC, D])
        got = sb("got", [P, TILES, K2, D])
        most = sb("most", [P, 1])
        mostu = sb("mostu", [P, 1], U32)
        wover = sb("wover", [P, TILES, E])
        overh = hT[:].rearrange("p a f s -> p (a f s)")[:, 0:FC * T].rearrange("p (f t) -> p f t", f=FC)

        ps = stack.enter_context(nc.psum_tensor("ps", [P, 8, 512], F32))
        BT, BNUM, BDEN = 4, 6, 7

        def weight(name):
            return sqw[:, W_NAMES.index(name), :]

        s_first = sem("first_loads")
        s_rows = sem("row_loads")
        s_zeroed = sem("zeroed")
        s_w = [sem(f"expert_weights{m}") for m in range(2)]
        s_set = sem("constants_set")
        s_iset = sem("ident_steps")
        s_dve = sem("dve_order")
        s_pool = sem("pool_order")
        s_act = sem("act_order")
        s_var = sem("variances")
        s_rstd = sem("rstd_ready")
        s_ctxn = sem("ctx_normed")
        s_ctxT = sem("ctx_transposed")
        s_kin = sem("kv_input")
        s_kv = sem("kv_projected")
        s_kvsb = sem("kv_in_sbuf")
        s_kvfree = sem("kv_banks_read")
        s_norm = sem("tokens_normed")
        s_inTp = sem("tokens_transposed")
        s_inT = sem("tokens_T_in_sbuf")
        s_q = sem("q_projected")
        s_qsb = sem("q_in_sbuf")
        s_sc = [sem(f"scores{m}") for m in range(2)]
        s_scfree = [sem("scores_read0")]
        s_shift = [sem(f"shifted{m}") for m in range(2)]
        s_exp = [sem(f"probs{m}") for m in range(2)]
        s_pt = [sem(f"probs_transposed{m}") for m in range(2)]
        s_ptsb = [sem(f"probsT_in_sbuf{m}") for m in range(2)]
        s_pv = [sem(f"attended{m}") for m in range(2)]
        s_att = [sem(f"attT_ready{m}") for m in range(2)]
        s_yTp = sem("yT_projected")
        s_yT = sem("yT_in_sbuf")
        s_yz = sem("y_projected")
        s_yzfree = sem("y_read")
        s_z = sem("gate_projected")
        s_zsb = sem("gate_in_sbuf")
        s_tanh = sem("gate_tanh")
        s_base = sem("base_ready")
        s_hid = [sem(f"moe_input{m}") for m in range(2)]
        s_hTp = [sem(f"moe_input_T{m}") for m in range(2)]
        s_hTsb = [sem(f"moe_input_T_sbuf{m}") for m in range(2)]
        s_log = [sem(f"logits{m}") for m in range(2)]
        s_dif = [sem(f"weight_difference{m}") for m in range(2)]
        s_wexp = [sem(f"weight_exp{m}") for m in range(2)]
        s_pick = [sem(f"picked{m}") for m in range(2)]
        s_rank = [sem(f"ranks{m}") for m in range(2)]
        s_slot = [sem(f"slots{m}") for m in range(2)]
        s_sent = [sem(f"rows_sent{m}") for m in range(2)]
        s_xe = [sem(f"expert_rows{e}") for e in range(E)]
        s_xT = [sem(f"expert_rows_T{m}") for m in range(2)]
        s_xTsb = [sem(f"expert_rows_T_sbuf{m}") for m in range(2)]
        s_up = [sem(f"expert_up{m}") for m in range(2)]
        s_silu = [sem(f"expert_silu{m}") for m in range(2)]
        s_down = [sem(f"expert_down{m}") for m in range(2)]
        s_ye = [sem(f"expert_out{m}") for m in range(2)]
        s_back = [sem(f"rows_back{m}") for m in range(2)]
        s_got = [sem(f"rows_gathered{t}") for t in range(TILES)]
        s_sum = [sem(f"block_sum{m}") for m in range(2)]
        s_most = sem("fullest_expert")
        s_oorder = sem("overflow_order")
        s_oup = sem("overflow_up")
        s_osilu = sem("overflow_silu")
        s_odown = sem("overflow_down")
        s_osum = sem("overflow_summed")
        s_out = sem("output_written")

        FIRST = 16 * 6
        CAP = [SLOT, CAP_D]

        def tiles(b):
            return range(TB * b, TB * b + TB)

        def chunk_rows(cap, c):
            return min(P, cap - P * c)

        def overflows(eng):
            eng.wait_ge(s_most, 1)
            return eng.If(eng.value_load(mostu[0:1, 0:1], min_val=0, max_val=B * T) > SLOT)

        block = stack.enter_context(nc.Block())

        @block.sync
        def _(sp):
            sp.dma_start(ctxs[:], ctx.rearrange("b k d -> k b d")).then_inc(s_first, 16)
            sp.dma_start(cst[:], consts).then_inc(s_first, 16)
            xt = x.rearrange("b (t p) d -> p (b t) d", p=P)
            sp.dma_start(xres[:, 0:TB, :], xt[:, 0:TB, :]).then_inc(s_first, 16)
            sp.dma_start(xres[:, TB:, :], xt[:, TB:, :]).then_inc(s_first, 16)
            sp.dma_start(col[:], cols).then_inc(s_first, 16)
            sp.dma_start(sqw[:], sq.rearrange("p (n d) -> p n d", d=D)).then_inc(s_first, 16)
            sp.dma_start(row[:], rows.broadcast_to([P, R_END])).then_inc(s_rows, 16)
            sp.dma_start(router[:, 0, :], wg).then_inc(s_rows, 16)
            sp.dma_start(router[:, 1, :], wr).then_inc(s_rows, 16)
            sp.dma_start(w1[:], w1b.rearrange("p (e f) -> p e f", e=E)).then_inc(s_w[0], 16)
            sp.dma_start(w2[:], w2b.rearrange("p (e c d) -> p e c d", e=E, c=FC)).then_inc(s_w[0], 16)
            sp.wait_ge(s_set, 1)
            for m in range(2):
                for e in range(E):
                    sp.dma_start(sent[m][e * SLOT:(e + 1) * SLOT, :].rearrange("(c p) d -> p c d", p=P),
                                 zero[:]).then_inc(s_zeroed, 16)
                sp.dma_start(back[m][NSLOT:NSLOT + 1, :], zero[0:1, 0, :]).then_inc(s_zeroed, 16)
            for m in range(2):
                sp.wait_ge(s_sent[m], 16 * TILES * K2)
                for e in range(E):
                    if m == 1 and e == 0:
                        sp.wait_ge(s_xT[0], E)
                    sp.dma_start(xe[:, e, :, :], sent[m][e * SLOT:(e + 1) * SLOT, :]
                                 .rearrange("(c p) d -> p c d", p=P)).then_inc(s_xe[e], 16)
                for e in range(E):
                    sp.wait_ge(s_ye[m], e + 1)
                    sp.dma_start(back[m][e * SLOT:(e + 1) * SLOT, :].rearrange("(c p) d -> p c d", p=P),
                                 ye[:, e, :, :]).then_inc(s_back[m], 16)
                if m == 0:
                    sp.wait_ge(s_down[0], E)
                    sp.wait_ge(s_sum[0], 1)
                    sp.dma_start(w1[:], w1d.rearrange("p (e f) -> p e f", e=E)).then_inc(s_w[1], 16)
                    sp.dma_start(w2[:], w2d.rearrange("p (e c d) -> p e c d", e=E, c=FC)).then_inc(s_w[1], 16)
            ot = out.rearrange("b (t p) d -> p (b t) d", p=P)
            for b in range(B):
                sp.wait_ge(s_sum[1], TB * (b + 1))
                sp.dma_start(ot[:, TB * b:TB * b + TB, :], xres[:, TB * b:TB * b + TB, :]).then_inc(s_out, 16)
            sp.wait_ge(s_out, 16 * B)

        @block.gpsimd
        def _(pool):
            pool.memset(zero[:], 0.0).then_inc(s_set, 1)
            pool.memset(power[:], -0.5).then_inc(s_iset, 1)
            pool.memset(ident[:], 0.0).then_inc(s_iset, 1)
            pool.memset(tri[:], 1.0).then_inc(s_iset, 1)
            pool.memset(ones[:], 1.0).then_inc(s_iset, 1)
            pool.memset(onepad[:], 0.0).then_inc(s_iset, 1)
            pool.memset(vpad[:], 0.0).then_inc(s_iset, 1)
            pool.wait_ge(s_iset, 6)
            pool.affine_select(out=ident[:], in_=ident[:], compare_op=ALU.not_equal, fill=1.0, base=0,
                               pattern=[[-1, P]], channel_multiplier=1).then_inc(s_set, 1)
            pool.affine_select(out=tri[:], in_=tri[:], compare_op=ALU.is_gt, fill=0.0, base=0,
                               pattern=[[1, P]], channel_multiplier=-1).then_inc(s_set, 1)
            for j in range(4):
                pool.memset(onepad[:, j, DH * j:DH * j + DH], 1.0).then_inc(s_set, 1)

            step = [0]

            def deviations(n, var, parts=P):
                pool.wait_ge(s_var, n)
                pool.tensor_scalar_add(vare[0:parts, var], mv[0:parts, var, 1], EPS).then_inc(s_pool, 1)
                step[0] += 1
                pool.wait_ge(s_pool, step[0])
                pool.tensor_tensor(rstd[0:parts, var], vare[0:parts, var], power[0:parts, var],
                                   ALU.pow).then_inc(s_rstd, 1)

            def send(m, b):
                pool.wait_ge(s_slot[m], b + 1)
                if b == 0:
                    pool.wait_ge(s_zeroed, 16 * 2 * (E + 1))
                for t in tiles(b):
                    for k in range(K2):
                        pool.indirect_dma_start(
                            sent[m], bass.IndirectOffsetOnAxis(ap=slotu[:, t, k:k + 1], axis=0),
                            hid[:, t, :], None, bounds_check=NSLOT - 1, oob_is_err=False).then_inc(s_sent[m], 16)

            def fetch(m):
                pool.wait_ge(s_back[m], 16 * E)
                if m == 1:
                    pool.wait_ge(s_sum[0], TILES)
                for t in range(TILES):
                    for k in range(K2):
                        pool.indirect_dma_start(
                            got[:, t, k, :], None, back[m],
                            bass.IndirectOffsetOnAxis(ap=slotu[:, t, k:k + 1], axis=0)).then_inc(s_got[t], 16)

            groups = [0]

            def next_group():
                groups[0] += 1
                return groups[0]

            deviations(next_group(), slice(0, B), KV)
            for b in range(B):
                g = slice(TB * b, TB * b + TB)
                deviations(next_group(), g)
                pool.wait_ge(s_hid[0], b + 1)
                pool.tensor_tensor(base[:, g, :], xres[:, g, :], hid[:, g, :], ALU.add).then_inc(s_base, 1)
                deviations(next_group(), g)
            for b in range(B):
                deviations(next_group(), slice(TB * b, TB * b + TB))
                send(0, b)
            fetch(0)
            for b in range(B):
                deviations(next_group(), slice(TB * b, TB * b + TB))
            for b in range(B):
                g = slice(TB * b, TB * b + TB)
                deviations(next_group(), g)
                send(1, b)
                pool.wait_ge(s_hid[1], b + 1)
                pool.tensor_tensor(base[:, g, :], xres[:, g, :], hid[:, g, :], ALU.add).then_inc(s_base, 1)
            fetch(1)

        @block.scalar
        def _(act):
            def attention(a, b):
                for u in range(UB * b, UB * b + UB + 1):
                    if u < UB * b + UB:
                        act.wait_ge(s_shift[a], u + 1)
                        if u >= 2:
                            act.wait_ge(s_pt[a], 2 * (u - 1))
                        act.activation(probs[:, u % 2], shifted[:, u % 2], ACT.Exp).then_inc(s_exp[a], 1)
                    if u > UB * b:
                        v = u - 1
                        t, half = v // 2, v % 2
                        pair = t // 2
                        if pair >= 2:
                            act.wait_ge(s_pv[a], pair - 1)
                        for i in range(2):
                            act.wait_ge(s_pt[a], 2 * v + i + 1)
                            h0 = HALF * half + HB * i
                            act.copy(probT[:, pair % 2, h0:h0 + HB, P * (t % 2):P * (t % 2) + P],
                                     ps[0:KV, BT + i, :].rearrange("p (h q) -> p h q", h=HB)).then_inc(s_ptsb[a], 1)

            def weights_exp(m, b):
                act.wait_ge(s_dif[m], b + 1)
                act.activation(wexp[:, TB * b:TB * b + TB], wdif[:, TB * b:TB * b + TB], ACT.Exp).then_inc(s_wexp[m], 1)

            def experts(m):
                for e in range(E):
                    for f in range(FC):
                        n = FC * e + f
                        act.wait_ge(s_up[m], n + 1)
                        if e >= 2:
                            act.wait_ge(s_down[m], e - 1)
                        bias = col[:, V_B1 + n:V_B1 + n + 1] if m == 0 else 0.0
                        act.activation(hT[:, e % 2, f, 0:CAP[m]], ps[:, 2 + n % 4, 0:CAP[m]], ACT.Silu,
                                       bias=bias).then_inc(s_silu[m], 1)

            act.wait_ge(s_first, FIRST)
            for b in range(B):
                attention(0, b)
                act.wait_ge(s_zsb, b + 1)
                act.activation(norm[:, TB * b:TB * b + TB, :], ztok[:], ACT.Tanh, scale=0.5).then_inc(s_tanh, 1)
                weights_exp(0, b)
            experts(0)
            with overflows(act):
                for e in range(E):
                    for b in range(B):
                        for f in range(FC):
                            n = B * e + b
                            act.wait_ge(s_oup, FC * n + f + 1)
                            if f == 0 and n >= 1:
                                act.wait_ge(s_odown, n)
                            act.activation(overh[:, f, :], ps[:, f, :], ACT.Silu,
                                           bias=col[:, V_B1 + FC * e + f:V_B1 + FC * e + f + 1]).then_inc(s_osilu, 1)
            for b in range(B):
                attention(1, b)
                weights_exp(1, b)
            experts(1)

        @block.vector
        def _(dve):
            order = {s_dve: 0, s_oorder: 0}

            def link(ins, on=s_dve):
                order[on] += 1
                ins.then_inc(on, 1)
                dve.wait_ge(on, order[on])

            group = [0]

            def variances(src, n, at, parts=P):
                for k in range(n):
                    last = dve.bn_stats(stats[0:parts, at + k, :], src[:, k, :])
                link(last)
                for k in range(n):
                    last = dve.bn_aggr(mv[0:parts, at + k, :], stats[0:parts, at + k, :])
                last.then_inc(s_var, 1)
                group[0] += 1
                dve.wait_ge(s_rstd, group[0])

            def normed(dst, src, n, at, parts=P):
                for k in range(n):
                    last = dve.tensor_scalar(dst[:, k, :], src[:, k, :], mv[0:parts, at + k, 0:1],
                                             rstd[0:parts, at + k:at + k + 1], ALU.subtract, ALU.mult)
                return last

            def attention(a, b):
                for u in range(UB * b, UB * b + UB):
                    t = (u // 2) % TB
                    s = ps[:, 2 * (u % 2):2 * (u % 2) + 2, 0:HB * KV].rearrange("p i (h k) -> p i h k", h=HB)
                    dst = shifted[:, u % 2]
                    dve.wait_ge(s_sc[a], u + 1)
                    if u >= 2:
                        dve.wait_ge(s_exp[a], u - 1)
                    if a == 0:
                        bias = cst[:, C_BIAS + t * KV:C_BIAS + (t + 1) * KV]
                        for i in range(2):
                            last = dve.tensor_tensor(dst[:, i], s[:, i], bias.unsqueeze(1).broadcast_to([P, HB, KV]), ALU.add)
                        last.then_inc(s_scfree[a], 1)
                        dve.wait_ge(s_scfree[a], u + 1)
                        s = dst
                    link(dve.tensor_reduce(peak[:, u % 2], s, AX.X, ALU.max))
                    last = dve.tensor_tensor(dst, s, peak[:, u % 2].unsqueeze(3).broadcast_to([P, 2, HB, KV]),
                                             ALU.subtract)
                    last.then_inc(s_shift[a], 1)

            def attended(a, b):
                dve.wait_ge(s_pv[a], 2 * (b + 1))
                link(dve.reciprocal(rden[:], ps[:, BDEN, :]))
                dve.tensor_tensor(attT[:, b, :], ps[:, BNUM, :], rden[:], ALU.mult).then_inc(s_att[a], 1)

            def keys_and_values(a):
                dve.wait_ge(s_kv, a + 1)
                kp = ps[:, 6, 0:B * KV].rearrange("p (b k) -> p b k", b=B)
                if a == 0:
                    kr = ps[:, 6, 256:256 + B * KV].rearrange("p (b k) -> p b k", b=B)
                    cos = cst[:, C_COS:C_COS + KV].unsqueeze(1).broadcast_to([P, B, KV])
                    sin = cst[:, C_SIN:C_SIN + KV].unsqueeze(1).broadcast_to([P, B, KV])
                    link(dve.tensor_tensor(kT[:], kp, cos, ALU.mult))
                    link(dve.tensor_tensor(ropek[:], kr, sin, ALU.mult))
                    link(dve.tensor_tensor(kT[:], kT[:], ropek[:], ALU.add))
                else:
                    link(dve.tensor_scalar(kT[:], kp, col[:, V_BK:V_BK + 1], None, ALU.add))
                mask = cst[:, C_MASK:C_MASK + H].unsqueeze(2).broadcast_to([P, H, KV])
                for b in range(B):
                    dve.tensor_tensor(kbd[:, b], kT[:, b, :].unsqueeze(1).broadcast_to([P, H, KV]), mask, ALU.mult)
                if a == 0:
                    dve.wait_ge(s_iset, 6)
                for b in range(B):
                    v = ps[0:KV, 7, b * D:(b + 1) * D].rearrange("p (g j d) -> p g j d", g=4, j=4)
                    for j in range(4):
                        dst = vpad[:, b, j:H:4, DH * j:DH * j + DH]
                        if a == 0:
                            last = dve.tensor_copy(dst, v[:, :, j, :])
                        else:
                            bv = row[0:KV, R_BV:R_BV + D].rearrange("p (g j d) -> p g j d", g=4, j=4)
                            last = dve.tensor_tensor(dst, v[:, :, j, :], bv[:, :, j, :], ALU.add)
                last.then_inc(s_kvsb, 1)

            def queries(a, b):
                dve.wait_ge(s_q, B * a + b + 1)
                if a == 0:
                    link(dve.tensor_tensor(qT[:, b, :], ps[:, 2 * b, :], cst[:, C_COS:C_COS + T], ALU.mult))
                    link(dve.tensor_tensor(ropeb[:], ps[:, 2 * b + 1, :], cst[:, C_SIN:C_SIN + T], ALU.mult))
                    dve.tensor_tensor(qT[:, b, :], qT[:, b, :], ropeb[:], ALU.add).then_inc(s_qsb, 1)
                else:
                    dve.tensor_scalar(qT[:, b, :], ps[:, 2 * b, :], col[:, V_BQ:V_BQ + 1], None, ALU.add)\
                       .then_inc(s_qsb, 1)

            def route(m, b):
                g = slice(TB * b, TB * b + TB)
                variances(xres[:, g, :], TB, TB * b)
                last = normed(hid[:, g, :], xres[:, g, :], TB, TB * b)
                last.then_inc(s_hid[m], 1)
                dve.wait_ge(s_hTp[m], b + 1)
                dve.tensor_copy(inT[:, b, :], ps[:, 4, :]).then_inc(s_hTsb[m], 1)
                dve.wait_ge(s_log[m], b + 1)
                lp = ps[:, 5, 0:TB * E].rearrange("p (t e) -> p t e", t=TB)
                if m == 0:
                    dve.wait_ge(s_rows, 48)
                    bg = row[:, R_BG:R_BG + E].unsqueeze(1).broadcast_to([P, TB, E])
                    link(dve.tensor_tensor(logit[:, g, :], lp, bg, ALU.add))
                    link(dve.tensor_scalar(logit[:, g, :], logit[:, g, :], GATE_DIV, None, ALU.mult))
                else:
                    link(dve.tensor_copy(logit[:, g, :], lp))
                for t in tiles(b):
                    last = dve.max(top[:, t, :], logit[:, t, :])
                link(last)
                for t in tiles(b):
                    last = dve.max_index(topi[:, t, :], top[:, t, :], logit[:, t, :])
                dve.tensor_tensor(wdif[:, g], top[:, g, 1], top[:, g, 0], ALU.subtract).then_inc(s_dif[m], 1)
                link(last)
                link(dve.tensor_copy(topf[:, g, :], topi[:, g, 0:K2]))
                iota = cst[:, C_IOTA:C_IOTA + E].unsqueeze(1).unsqueeze(1).broadcast_to([P, TB, K2, E])
                link(dve.tensor_tensor(pick[:, g], topf[:, g, :].unsqueeze(3).broadcast_to([P, TB, K2, E]), iota,
                                       ALU.is_equal))
                dve.tensor_tensor(picked[:, g, :], pick[:, g, 0, :], pick[:, g, 1, :], ALU.add).then_inc(s_pick[m], 1)
                dve.wait_ge(s_wexp[m], b + 1)
                link(dve.tensor_scalar(wden[:, g], wexp[:, g], 1.0, None, ALU.add))
                link(dve.reciprocal(wtok[:, g, 0], wden[:, g]))
                link(dve.tensor_tensor(wtok[:, g, 1], wexp[:, g], wtok[:, g, 0], ALU.mult))
                dve.wait_ge(s_rank[m], b + 1)
                rp = ps[:, 7, TB * b * E:(TB * b + TB) * E].rearrange("p (t e) -> p t e", t=TB)
                link(dve.tensor_tensor(ranked[:, g], pick[:, g], rp.unsqueeze(2).broadcast_to([P, TB, K2, E]), ALU.mult))
                link(dve.tensor_reduce(rank[:, g, :], ranked[:, g], AX.X, ALU.add))
                if m == 0 and b == B - 1:
                    link(dve.tensor_reduce(most[:], ps[:, 7, TILES * E:TILES * E + E], AX.X, ALU.max))
                    dve.tensor_copy(mostu[:], most[:]).then_inc(s_most, 1)
                link(dve.tensor_scalar(over[:, g, :], rank[:, g, :], float(CAP[m]), float(NSLOT), ALU.is_ge, ALU.mult))
                link(dve.scalar_tensor_tensor(out=slot[:, g, :], in0=topf[:, g, :], scalar=float(SLOT),
                                              in1=rank[:, g, :], op0=ALU.mult, op1=ALU.add))
                link(dve.tensor_tensor(slot[:, g, :], slot[:, g, :], over[:, g, :], ALU.add))
                dve.tensor_scalar(slotu[:, g, :], slot[:, g, :], float(NSLOT), None, ALU.min).then_inc(s_slot[m], 1)

            def experts(m):
                for e in range(E + 1):
                    if e < E:
                        dve.wait_ge(s_xT[m], e + 1)
                        if e >= 2:
                            dve.wait_ge(s_up[m], FC * (e - 1))
                        dve.tensor_copy(xeT[:, e % 2, 0:CAP[m]], ps[:, e % 2, 0:CAP[m]]).then_inc(s_xTsb[m], 1)
                    if e >= 1:
                        o = e - 1
                        dve.wait_ge(s_down[m], o + 1)
                        if m == 1 and o == 0:
                            dve.wait_ge(s_back[0], 16 * E)
                        for c in range(SC):
                            n = chunk_rows(CAP[m], c)
                            src = ps[0:n, 6 + o % 2, c * P:(c + 1) * P]
                            if m == 0:
                                last = dve.tensor_tensor(ye[0:n, o, c, :], src,
                                                         row[0:n, R_B2 + o * D:R_B2 + (o + 1) * D], ALU.add)
                            else:
                                last = dve.tensor_copy(ye[0:n, o, c, :], src)
                        last.then_inc(s_ye[m], 1)

            def combine(m, t):
                src = xres if m == 0 else base
                dve.wait_ge(s_got[t], 16 * K2 * (m + 1))
                if m == 1 and t % TB == 0:
                    dve.wait_ge(s_base, B + t // TB + 1)
                link(dve.scalar_tensor_tensor(out=norm[:, t, :], in0=got[:, t, 0, :], scalar=wtok[:, t, 0:1],
                                              in1=src[:, t, :], op0=ALU.mult, op1=ALU.add))
                last = dve.scalar_tensor_tensor(out=xres[:, t, :], in0=got[:, t, 1, :], scalar=wtok[:, t, 1:2],
                                                in1=norm[:, t, :], op0=ALU.mult, op1=ALU.add)
                last.then_inc(s_sum[m], 1)

            dve.wait_ge(s_first, FIRST)
            variances(ctxs[:], B, 0, KV)
            normed(ctxn[:], ctxs[:], B, 0, KV).then_inc(s_ctxn, 1)
            dve.wait_ge(s_ctxT, 1)
            dve.tensor_scalar(kinT[:], ps[:, 0, 0:B * KV].rearrange("p (b k) -> p b k", b=B),
                              col[:, V_GAMMA:V_GAMMA + 1], col[:, V_BETA:V_BETA + 1], ALU.mult, ALU.add)\
               .then_inc(s_kin, 1)
            for b in range(B):
                g = slice(TB * b, TB * b + TB)
                variances(xres[:, g, :], TB, TB * b)
                last = normed(hid[:, g, :], xres[:, g, :], TB, TB * b)
                last.then_inc(s_hid[0], 1)
                dve.wait_ge(s_hid[0], b + 1)
                variances(hid[:, g, :], TB, TB * b)
                normed(norm[:, g, :], hid[:, g, :], TB, TB * b).then_inc(s_norm, 1)
                if b == 0:
                    keys_and_values(0)
                dve.wait_ge(s_inTp, b + 1)
                dve.tensor_scalar(inT[:, b, :], ps[:, 4 + b, :], col[:, V_GAMMA:V_GAMMA + 1],
                                  col[:, V_BETA:V_BETA + 1], ALU.mult, ALU.add).then_inc(s_inT, 1)
                queries(0, b)
            dve.wait_ge(s_rows, 48)
            for b in range(B):
                g = slice(TB * b, TB * b + TB)
                attention(0, b)
                attended(0, b)
                dve.wait_ge(s_yTp, b + 1)
                dve.tensor_scalar(yT[:], ps[:, 4, :], col[:, V_BOUT:V_BOUT + 1], None, ALU.add).then_inc(s_yT, 1)
                dve.wait_ge(s_yz, b + 1)
                bout = row[:, R_BOUT:R_BOUT + D].unsqueeze(1).broadcast_to([P, TB, D])
                bgate = row[:, R_BGATE:R_BGATE + D].unsqueeze(1).broadcast_to([P, TB, D])
                link(dve.tensor_tensor(ytok[:], ps[:, 0, :].rearrange("p (t d) -> p t d", t=TB), bout, ALU.add))
                link(dve.tensor_tensor(ytok[:], ytok[:], hid[:, g, :], ALU.subtract))
                dve.wait_ge(s_z, b + 1)
                dve.tensor_tensor(ztok[:], ps[:, 1, :].rearrange("p (t d) -> p t d", t=TB), bgate, ALU.add)\
                   .then_inc(s_zsb, 1)
                dve.wait_ge(s_tanh, b + 1)
                link(dve.scalar_tensor_tensor(out=ytok[:], in0=norm[:, g, :], scalar=1.0, in1=ytok[:],
                                              op0=ALU.add, op1=ALU.mult))
                dve.wait_ge(s_base, b + 1)
                link(dve.scalar_tensor_tensor(out=xres[:, g, :], in0=ytok[:], scalar=0.5, in1=base[:, g, :],
                                              op0=ALU.mult, op1=ALU.add))
                route(0, b)
            experts(0)
            with overflows(dve):
                link(dve.tensor_tensor(ranked[:], pick[:], over[:].unsqueeze(3).broadcast_to([P, TILES, K2, E]),
                                       ALU.mult), s_oorder)
                link(dve.tensor_tensor(ranked[:], ranked[:], wtok[:].unsqueeze(3).broadcast_to([P, TILES, K2, E]),
                                       ALU.mult), s_oorder)
                link(dve.tensor_tensor(wover[:], ranked[:, :, 0, :], ranked[:, :, 1, :], ALU.add), s_oorder)
                link(dve.tensor_scalar(wover[:], wover[:], 1.0 / NSLOT, None, ALU.mult), s_oorder)
                for e in range(E):
                    b2 = row[:, R_B2 + e * D:R_B2 + (e + 1) * D].unsqueeze(1).broadcast_to([P, TB, D])
                    for b in range(B):
                        dve.wait_ge(s_odown, B * e + b + 1)
                        dve.tensor_tensor(ytok[:], ps[:, 4, :].rearrange("p (t d) -> p t d", t=TB), b2, ALU.add)\
                           .then_inc(s_osum, 1)
                        dve.wait_ge(s_osum, B * e + b + 1)
                        for k in range(TB):
                            t = TB * b + k
                            last = dve.scalar_tensor_tensor(out=xres[:, t, :], in0=ytok[:, k, :], scalar=wover[:, t, e:e + 1],
                                                            in1=xres[:, t, :], op0=ALU.mult, op1=ALU.add)
                        link(last, s_oorder)
            for t in range(TILES):
                combine(0, t)
                if t % TB == TB - 1:
                    b = t // TB
                    g = slice(TB * b, TB * b + TB)
                    dve.wait_ge(s_sum[0], t + 1)
                    variances(xres[:, g, :], TB, TB * b)
                    normed(norm[:, g, :], xres[:, g, :], TB, TB * b).then_inc(s_norm, 1)
            dve.wait_ge(s_ctxT, 2)
            dve.tensor_copy(kinT[:], ps[:, 0, 0:B * KV].rearrange("p (b k) -> p b k", b=B)).then_inc(s_kin, 1)
            keys_and_values(1)
            for b in range(B):
                dve.wait_ge(s_inTp, B + b + 1)
                dve.tensor_copy(inT[:, b, :], ps[:, 4 + b, :]).then_inc(s_inT, 1)
                queries(1, b)
            for b in range(B):
                g = slice(TB * b, TB * b + TB)
                attention(1, b)
                attended(1, b)
                dve.wait_ge(s_yz, B + b + 1)
                bo = row[:, R_BO:R_BO + D].unsqueeze(1).broadcast_to([P, TB, D])
                link(dve.tensor_tensor(ytok[:], ps[:, 0, :].rearrange("p (t d) -> p t d", t=TB), bo, ALU.add))
                link(dve.tensor_tensor(xres[:, g, :], xres[:, g, :], ytok[:], ALU.add))
                route(1, b)
            experts(1)
            for t in range(TILES):
                combine(1, t)

        @block.tensor
        def _(pe):
            def transposed(bank, src, n, parts=P):
                for k in range(n):
                    last = pe.matmul(ps[:, bank, k * parts:(k + 1) * parts], src(k), ident[0:parts, 0:parts],
                                     start=True, stop=True, is_transpose=True)
                return last

            def scores(a, u):
                b, t = u // UB, (u // 2) % TB
                if u >= 2:
                    pe.wait_ge(s_scfree[0] if a == 0 else s_shift[1], u - 1)
                for i in range(2):
                    h0 = HALF * (u % 2) + HB * i
                    last = pe.matmul(ps[:, 2 * (u % 2) + i, 0:HB * KV], qT[:, b, t * P:(t + 1) * P],
                                     kbd[:, b, h0:h0 + HB, :].rearrange("p h k -> p (h k)"), start=True, stop=True)
                last.then_inc(s_sc[a], 1)

            def transpose_probs(a, u):
                pe.wait_ge(s_exp[a], u + 1)
                for i in range(2):
                    if u >= 1:
                        pe.wait_ge(s_ptsb[a], 2 * (u - 1) + i + 1)
                    for h in range(HB):
                        last = pe.matmul(ps[0:KV, BT + i, h * P:(h + 1) * P], probs[:, u % 2, i, h, :], ident[:],
                                         start=True, stop=True, is_transpose=True)
                    last.then_inc(s_pt[a], 1)

            def attend(a, pair):
                b = pair // 2
                pe.wait_ge(s_ptsb[a], 8 * (pair + 1))
                q = slice(PAIR * (pair % 2), PAIR * (pair % 2) + PAIR)
                for bank, lhs in ((BNUM, None), (BDEN, onepad)):
                    for j in range(4):
                        for g in range(4):
                            h = 4 * g + j
                            w = vpad[:, b, h, :] if lhs is None else lhs[:, j, :]
                            last = pe.matmul(ps[32 * g:32 * g + 32, bank, q], w, probT[:, pair % 2, h, :],
                                             start=(j == 0), stop=(j == 3))
                last.then_inc(s_pv[a], 1)

            def attention(a, b):
                u0 = UB * b
                if b == 1:
                    pe.wait_ge(s_att[a], b)
                scores(a, u0)
                for u in range(u0, u0 + UB):
                    if u + 1 < u0 + UB:
                        scores(a, u + 1)
                    transpose_probs(a, u)
                    if u == u0 + 4:
                        attend(a, 2 * b)
                attend(a, 2 * b + 1)

            def route(m, b):
                pe.wait_ge(s_hid[m], (B if m == 0 else 0) + b + 1)
                transposed(4, lambda k: hid[:, TB * b + k, :], TB).then_inc(s_hTp[m], 1)
                pe.wait_ge(s_hTsb[m], b + 1)
                if m == 0:
                    pe.wait_ge(s_rows, 48)
                for k in range(TB):
                    last = pe.matmul(ps[:, 5, k * E:(k + 1) * E], inT[:, b, k * P:(k + 1) * P], router[:, m, :],
                                     start=True, stop=True)
                last.then_inc(s_log[m], 1)
                pe.wait_ge(s_pick[m], b + 1)
                for t in tiles(b):
                    for s in range(t + 1):
                        last = pe.matmul(ps[:, 7, t * E:(t + 1) * E], tri[:] if s == t else ones[:], picked[:, s, :],
                                         start=(s == 0), stop=(s == t))
                if m == 0 and b == B - 1:
                    for t in range(TILES):
                        last = pe.matmul(ps[:, 7, TILES * E:TILES * E + E], ones[:], picked[:, t, :],
                                         start=(t == 0), stop=(t == TILES - 1))
                last.then_inc(s_rank[m], 1)

            def experts(m):
                cap = CAP[m]
                pe.wait_ge(s_w[m], 32)
                pe.wait_ge(s_slot[m], B)

                def rows_in(e):
                    pe.wait_ge(s_xe[e], 16 * (m + 1))
                    if e >= 2:
                        pe.wait_ge(s_xTsb[m], e - 1)
                    for c in range(SC):
                        n = chunk_rows(cap, c)
                        last = pe.matmul(ps[:, e % 2, c * P:c * P + n], xe[0:n, e, c, :], ident[0:n, 0:n],
                                         start=True, stop=True, is_transpose=True)
                    last.then_inc(s_xT[m], 1)

                def up(e):
                    pe.wait_ge(s_xTsb[m], e + 1)
                    for f in range(FC):
                        n = FC * e + f
                        if n >= 4:
                            pe.wait_ge(s_silu[m], n - 3)
                        pe.matmul(ps[:, 2 + n % 4, 0:cap], w1[:, e, f * P:(f + 1) * P], xeT[:, e % 2, 0:cap],
                                  start=True, stop=True).then_inc(s_up[m], 1)

                def down(e):
                    pe.wait_ge(s_silu[m], FC * (e + 1))
                    if e >= 2:
                        pe.wait_ge(s_ye[m], e - 1)
                    for c in range(SC):
                        n = chunk_rows(cap, c)
                        for f in range(FC):
                            last = pe.matmul(ps[0:n, 6 + e % 2, c * P:(c + 1) * P], hT[:, e % 2, f, c * P:c * P + n],
                                             w2[:, e, f, :], start=(f == 0), stop=(f == FC - 1))
                    last.then_inc(s_down[m], 1)

                rows_in(0)
                for e in range(E + 1):
                    if e + 1 < E:
                        rows_in(e + 1)
                    if e < E:
                        up(e)
                    if e >= 1:
                        down(e - 1)

            def project_kv(a):
                pe.wait_ge(s_kin, a + 1)
                names = (("k0", 0), ("k0p", 256)) if a == 0 else (("k1", 0),)
                for name, at in names:
                    pe.matmul(ps[:, 6, at:at + B * KV], weight(name), kinT[:].rearrange("p b k -> p (b k)"),
                              start=True, stop=True)
                for b in range(B):
                    last = pe.matmul(ps[0:KV, 7, b * D:(b + 1) * D], kinT[:, b, :], weight(f"v{a}"),
                                     start=True, stop=True)
                last.then_inc(s_kv, 1)

            def project_q(a, b):
                pe.wait_ge(s_norm, B * a + b + 1)
                transposed(4 + b, lambda k: norm[:, TB * b + k, :], TB).then_inc(s_inTp, 1)
                pe.wait_ge(s_inT, B * a + b + 1)
                last = pe.matmul(ps[:, 2 * b, :], weight(f"q{a}"), inT[:, b, :], start=True, stop=True)
                if a == 0:
                    last = pe.matmul(ps[:, 2 * b + 1, :], weight("q0p"), inT[:, b, :], start=True, stop=True)
                last.then_inc(s_q, 1)

            pe.wait_ge(s_first, FIRST)
            pe.wait_ge(s_set, 7)
            pe.wait_ge(s_ctxn, 1)
            transposed(0, lambda k: ctxn[:, k, :], B, KV).then_inc(s_ctxT, 1)
            project_kv(0)
            for b in range(B):
                project_q(0, b)
            pe.wait_ge(s_qsb, B)
            pe.wait_ge(s_kvsb, 1)
            for b in range(B):
                attention(0, b)
                pe.wait_ge(s_att[0], b + 1)
                pe.wait_ge(s_ptsb[0], 2 * UB * (b + 1))
                pe.matmul(ps[:, 4, :], weight("out0"), attT[:, b, :], start=True, stop=True).then_inc(s_yTp, 1)
                for k in range(TB):
                    last = pe.matmul(ps[:, 0, k * D:(k + 1) * D], attT[:, b, k * P:(k + 1) * P], weight("out0"),
                                     start=True, stop=True)
                last.then_inc(s_yz, 1)
                pe.wait_ge(s_yT, b + 1)
                for k in range(TB):
                    last = pe.matmul(ps[:, 1, k * D:(k + 1) * D], yT[:, k * P:(k + 1) * P], weight("gate0"),
                                     start=True, stop=True)
                last.then_inc(s_z, 1)
                route(0, b)
            experts(0)
            pe.wait_ge(s_ye[0], E)
            with overflows(pe):
                for e in range(E):
                    for b in range(B):
                        n = B * e + b
                        for f in range(FC):
                            if n >= 1:
                                pe.wait_ge(s_osilu, FC * (n - 1) + f + 1)
                            pe.matmul(ps[:, f, :], w1[:, e, f * P:(f + 1) * P], inT[:, b, :], start=True, stop=True)\
                              .then_inc(s_oup, 1)
                        pe.wait_ge(s_osilu, FC * (n + 1))
                        if n >= 1:
                            pe.wait_ge(s_osum, n)
                        for k in range(TB):
                            for f in range(FC):
                                last = pe.matmul(ps[:, 4, k * P:(k + 1) * P], overh[:, f, k * P:(k + 1) * P],
                                                 w2[:, e, f, :], start=(f == 0), stop=(f == FC - 1))
                        last.then_inc(s_odown, 1)
            transposed(0, lambda k: ctxs[:, k, :], B, KV).then_inc(s_ctxT, 1)
            project_kv(1)
            for b in range(B):
                project_q(1, b)
            pe.wait_ge(s_qsb, 2 * B)
            pe.wait_ge(s_kvsb, 2)
            for b in range(B):
                attention(1, b)
                pe.wait_ge(s_att[1], b + 1)
                for k in range(TB):
                    last = pe.matmul(ps[:, 0, k * D:(k + 1) * D], attT[:, b, k * P:(k + 1) * P], weight("o1"),
                                     start=True, stop=True)
                last.then_inc(s_yz, 1)
                pe.wait_ge(s_ptsb[1], 2 * UB * (b + 1))
                route(1, b)
            experts(1)


def partner(w):
    return w.reshape(D, H, 2, DH // 2)[:, :, ::-1, :].reshape(D, D)


def kernel(x, ctx_1024, L0_xattn_Wqkv, L0_xattn_Wout, L0_xattn_b_out, L0_xattn_Wgate, L0_xattn_b_gate,
           L0_xattn_gamma, L0_xattn_beta, L0_ffn_Wg, L0_ffn_bg, L0_ffn_W1, L0_ffn_b1, L0_ffn_W2, L0_ffn_b2,
           L1_xattn_W_Q, L1_xattn_b_Q, L1_xattn_W_K, L1_xattn_b_K, L1_xattn_W_V, L1_xattn_b_V,
           L1_xattn_W_O, L1_xattn_b_O, L1_ffn_router_w, L1_ffn_w1, L1_ffn_w2):
    import concourse.bacc as bacc
    from concourse.bass_utils import run_bass_kernel_spmd

    a = {k: np.asarray(v) for k, v in locals().items() if k not in ("bacc", "run_bass_kernel_spmd")}
    wqkv = a["L0_xattn_Wqkv"]
    wq, wk, wv = wqkv[:D].T, wqkv[D:2 * D].T, wqkv[2 * D:].T
    square = [wq, partner(wq), wk, partner(wk), wv, a["L0_xattn_Wout"].T, a["L0_xattn_Wgate"].T,
              a["L1_xattn_W_Q"], a["L1_xattn_W_K"], a["L1_xattn_W_V"], a["L1_xattn_W_O"]]
    b1 = a["L0_ffn_b1"].reshape(E * FC, P).T
    cols = [a["L0_xattn_gamma"][:, None], a["L0_xattn_beta"][:, None], a["L0_xattn_b_out"][:, None],
            a["L1_xattn_b_Q"][:, None], a["L1_xattn_b_K"][:, None], b1]
    rows = [a["L0_xattn_b_out"], a["L0_xattn_b_gate"], a["L1_xattn_b_O"], a["L1_xattn_b_V"], a["L0_ffn_bg"],
            a["L0_ffn_b2"].reshape(-1)]

    def up(w):
        return w.transpose(1, 0, 2).reshape(P, E * FF)

    def down(w):
        return w.reshape(E, FC, P, D).transpose(2, 0, 1, 3).reshape(P, E * FC * D)

    arrays = {
        "x": a["x"], "ctx": a["ctx_1024"], "consts": constants(), "square": np.concatenate(square, axis=1),
        "cols": np.concatenate(cols, axis=1), "rows": np.concatenate(rows)[None, :],
        "wg": a["L0_ffn_Wg"], "wr": a["L1_ffn_router_w"].T,
        "w1b": up(a["L0_ffn_W1"]), "w2b": down(a["L0_ffn_W2"]),
        "w1d": up(a["L1_ffn_w1"]), "w2d": down(a["L1_ffn_w2"]),
    }
    arrays = {k: np.ascontiguousarray(v) for k, v in arrays.items()}
    nc = bacc.Bacc("TRN2", target_bir_lowering=False, num_devices=1)
    args = [nc.dram_tensor(k, v.shape, mybir.dt.from_np(v.dtype), kind="ExternalInput").ap() for k, v in arrays.items()]
    out = nc.dram_tensor("out", (B, T, D), mybir.dt.float32, kind="ExternalOutput").ap()
    two_block_kernel(nc, *args, out)
    r = run_bass_kernel_spmd(nc, [arrays], core_ids=[0])
    return r.results[0]["out"]
```

```python
import numpy as np
import concourse.bass as bass
from concourse import mybir
from contextlib import ExitStack

B, T, D = 2, 512, 128
KV = 77
H, DH = 16, 8
P = 128
TILES = B * T // P
TB = T // P
HALF = H // 2
UNITS = 2 * TILES
UB = 2 * TB
HB = HALF // 2
GT = 2
GROUPS = TILES // GT
GQ = GT * P
UG = 2 * GT
E, K2 = 8, 2
FF = 512
FC = FF // P
SLOT = 384
SC = SLOT // P
NSLOT = E * SLOT
NPAIR = B * T * K2
ROW = D + 1
CAP_D = int(1.25 * B * T * K2 / E) + 1
EPS = 1e-5
SCALE = DH ** -0.5
GATE_DIV = float(np.float32(1.0) / np.float32(1.0 + 1e-6))

C_COS, C_SIN, C_BIAS = 0, T, 2 * T
C_MASK = C_BIAS + TB * KV
C_IOTA = C_MASK + H
C_PAIR = C_IOTA + E
C_END = C_PAIR + TILES * K2
R_BOUT, R_BGATE, R_BO, R_BV, R_BG, R_B2 = 0, D, 2 * D, 3 * D, 4 * D, 4 * D + E
R_END = R_B2 + E * D
V_GAMMA, V_BETA, V_BOUT, V_BQ, V_BK, V_B1 = 0, 1, 2, 3, 4, 5
V_END = V_B1 + E * FC
W_NAMES = ["q0", "q0p", "k0", "k0p", "v0", "out0", "gate0", "q1", "k1", "v1", "o1"]


PE_STEPS = [dict(attend=1, project=2, gate=3, turn=6, logits=7, ranks=8),
            dict(attend=1, project=2, turn=4, logits=5, ranks=6)]
DVE_STEPS = [dict(attended=2, projected=3, gate=4, residual=5, hidden=6, choose=8, slots=9),
             dict(attended=2, residual=3, hidden=4, choose=6, slots=7)]
ACT_STEPS = [dict(tanh=4, turned=7, weights=8), dict(turned=5, weights=6)]


def due(steps, u):
    for name, delay in steps.items():
        g, rest = divmod(u - delay - (UG - 1), UG)
        if rest == 0 and 0 <= g < GROUPS:
            yield name, g


def resized_bias():
    n = 128
    pos = np.arange(n, dtype=np.float64)
    dist = np.abs(pos[None, :] - pos[:, None])
    bias = np.exp(-dist * 0.1) - dist * 0.05

    def weights(out):
        inv = n / out
        at = (np.arange(out) + 0.5) * inv - 0.5
        w = np.maximum(0.0, 1.0 - np.abs(at[None, :] - np.arange(n)[:, None]) / max(inv, 1.0))
        return w / w.sum(axis=0, keepdims=True)

    return (weights(T).T @ bias @ weights(KV)).astype(np.float32)


def constants():
    c = np.zeros((P, C_END), np.float32)
    half = DH // 2
    inv_freq = 1.0 / 10000.0 ** (np.arange(0, DH, 2, dtype=np.float32) / np.float32(DH))
    freqs = np.arange(T, dtype=np.float32)[:, None] * inv_freq.astype(np.float32)[None, :]
    lane = np.arange(P) % DH
    angle = freqs[:, lane % half].T.astype(np.float32)
    c[:, C_COS:C_COS + T] = np.cos(angle.astype(np.float64))
    c[:, C_SIN:C_SIN + T] = np.where(lane[:, None] < half, -1.0, 1.0) * np.sin(angle.astype(np.float64))
    bias = resized_bias().reshape(TB, P, KV)
    c[:, C_BIAS:C_BIAS + TB * KV] = bias.transpose(1, 0, 2).reshape(P, TB * KV)
    c[:, C_MASK:C_MASK + H] = SCALE * (np.arange(P)[:, None] // DH == np.arange(H)[None, :])
    c[:, C_IOTA:C_IOTA + E] = np.arange(E)[None, :]
    token = np.arange(TILES)[None, :, None] * P + np.arange(P)[:, None, None]
    c[:, C_PAIR:C_PAIR + TILES * K2] = (token * K2 + np.arange(K2)).reshape(P, TILES * K2)
    return c


def two_block_kernel(nc, x, ctx, consts, sq, cols, rows, wg, wr, w1b, w2b, w1d, w2d, out):
    F32, BF16, U32 = mybir.dt.float32, mybir.dt.bfloat16, mybir.dt.uint32
    ALU = mybir.AluOpType
    ACT = mybir.ActivationFunctionType
    AX = mybir.AxisListType

    with ExitStack() as stack:
        def sb(name, shape, dt=F32):
            return stack.enter_context(nc.sbuf_tensor(name, shape, dt))

        def sem(name):
            return stack.enter_context(nc.semaphore(name))

        sent = [nc.dram_tensor(f"sent{m}", (NSLOT, ROW), F32, kind="Internal").ap() for m in range(2)]
        back = [nc.dram_tensor(f"back{m}", (NPAIR, D), F32, kind="Internal").ap() for m in range(2)]

        cst = sb("cst", [P, C_END])
        sqw = sb("sqw", [P, len(W_NAMES), D])
        col = sb("col", [P, V_END])
        row = sb("row", [P, R_END])
        router = sb("router", [P, 2, E])
        w1 = sb("w1", [P, E, FF])
        w2 = sb("w2", [P, E, FC, D])
        blank = sb("blank", [P, SC, ROW])
        ident = sb("ident", [P, P])
        tri = sb("tri", [P, P], BF16)
        ones = sb("ones", [P, P], BF16)
        power = sb("power", [P, TILES])
        hidk = sb("hidk", [P, TILES, K2, ROW])
        hidb = sb("hidb", [P, TILES, D])
        pairu = sb("pairu", [P, E, SC], U32)
        xres = sb("xres", [P, TILES, D])
        hid = sb("hid", [P, TILES, D])
        base = sb("base", [P, TILES, D])
        norm = sb("norm", [P, TILES, D])
        ctxs = sb("ctxs", [KV, B, D])
        ctxn = sb("ctxn", [KV, B, D])
        stats = sb("stats", [P, TILES, 6])
        mv = sb("mv", [P, TILES, 2])
        vare = sb("vare", [P, TILES])
        rstd = sb("rstd", [P, TILES])
        inT = sb("inT", [P, B, T])
        kinT = sb("kinT", [P, B, KV])
        qT = sb("qT", [P, B, T])
        ropeb = sb("ropeb", [P, 2, GQ])
        kT = sb("kT", [P, B, KV])
        ropek = sb("ropek", [P, B, KV])
        kbd = sb("kbd", [P, B, H, KV])
        vpad = sb("vpad", [KV, B, H, 32])
        onepad = sb("onepad", [KV, 4, 32])
        shifted = sb("shifted", [P, 2, 2, HB, KV])
        probs = sb("probs", [P, 2, 2, HB, KV])
        peak = sb("peak", [P, 2, 2, HB])
        probT = sb("probT", [P, 2, H, GQ])
        attT = sb("attT", [P, B, T])
        rden = sb("rden", [P, GQ])
        yT = sb("yT", [P, GQ])
        ytok = sb("ytok", [P, TILES, D])
        ztok = sb("ztok", [P, GT, D])
        logit = sb("logit", [P, TILES, E])
        top = sb("top", [P, TILES, 8])
        topi = sb("topi", [P, TILES, 8], U32)
        topf = sb("topf", [P, TILES, K2])
        pick = sb("pick", [P, TILES, K2, E])
        picked = sb("picked", [P, TILES, E], BF16)
        ranked = sb("ranked", [P, TILES, K2, E])
        rank = sb("rank", [P, TILES, K2])
        slot = sb("slot", [P, TILES, K2])
        over = sb("over", [P, TILES, K2])
        slotu = sb("slotu", [P, TILES, K2], U32)
        wdif = sb("wdif", [P, TILES])
        wexp = sb("wexp", [P, TILES])
        wden = sb("wden", [P, TILES])
        wtok = sb("wtok", [P, TILES, K2])
        xe = sb("xe", [P, E, SC, ROW])
        xeT = sb("xeT", [P, 2, SLOT])
        hT = sb("hT", [P, 2, FC, SLOT])
        ye = probT[:].rearrange("p g h q -> p (g h q)")[:, 0:E * SC * D].rearrange("p (e c d) -> p e c d", e=E, c=SC)
        got = sb("got", [P, TILES, K2, D])
        most = sb("most", [P, 1])
        mostu = sb("mostu", [P, 1], U32)
        wover = sb("wover", [P, TILES, E])
        overh = hT[:].rearrange("p a f s -> p (a f s)")[:, 0:FC * T].rearrange("p (f t) -> p f t", f=FC)

        ps = stack.enter_context(nc.psum_tensor("ps", [P, 8, 512], F32))
        BT, BA, BR = 4, 6, 7

        def weight(name):
            return sqw[:, W_NAMES.index(name), :]

        s_ctx = sem("ctx_loaded")
        s_x = [sem(f"x_loaded{b}") for b in range(B)]
        s_sq = sem("square_weights_loaded")
        s_cst = sem("constants_loaded")
        s_h = sem("first_norm")
        s_rows = sem("row_loads")
        s_blank = [sem(f"blank_rows{m}") for m in range(2)]
        s_w = [sem(f"expert_weights{m}") for m in range(2)]
        s_set = sem("constants_set")
        s_iset = sem("ident_steps")
        s_dve = sem("dve_order")
        s_pool = sem("pool_order")
        s_act = sem("act_order")
        s_var = sem("variances")
        s_rstd = sem("rstd_ready")
        s_ctxn = sem("ctx_normed")
        s_ctxT = sem("ctx_transposed")
        s_kin = sem("kv_input")
        s_kv = sem("kv_projected")
        s_kvsb = sem("kv_in_sbuf")
        s_kvfree = sem("kv_banks_read")
        s_norm = sem("tokens_normed")
        s_inTp = sem("tokens_transposed")
        s_inT = sem("tokens_T_in_sbuf")
        s_q = sem("q_projected")
        s_qsb = sem("q_in_sbuf")
        s_sc = [sem(f"scores{m}") for m in range(2)]
        s_scfree = [sem("scores_read0")]
        s_shift = [sem(f"shifted{m}") for m in range(2)]
        s_exp = [sem(f"probs{m}") for m in range(2)]
        s_pt = [sem(f"probs_transposed{m}") for m in range(2)]
        s_ptsb = [sem(f"probsT_in_sbuf{m}") for m in range(2)]
        s_pv = [sem(f"attended{m}") for m in range(2)]
        s_att = [sem(f"attT_ready{m}") for m in range(2)]
        s_yTp = sem("yT_projected")
        s_yT = sem("yT_in_sbuf")
        s_yz = sem("y_projected")
        s_yzfree = sem("y_read")
        s_z = sem("gate_projected")
        s_zsb = sem("gate_in_sbuf")
        s_tanh = sem("gate_tanh")
        s_rope = sem("rope_parts")
        s_hbase = sem("residual_ready")
        s_hidk = [sem(f"moe_rows{m}") for m in range(2)]
        s_base = sem("base_ready")
        s_residual = [sem(f"residual{m}") for m in range(2)]
        s_pair = [sem(f"pair_numbers{m}") for m in range(2)]
        s_kvclear = sem("kv_buffers_clear")
        s_hid = [sem(f"moe_input{m}") for m in range(2)]
        s_hTp = [sem(f"moe_input_T{m}") for m in range(2)]
        s_hTsb = [sem(f"moe_input_T_sbuf{m}") for m in range(2)]
        s_log = [sem(f"logits{m}") for m in range(2)]
        s_dif = [sem(f"weight_difference{m}") for m in range(2)]
        s_wexp = [sem(f"weight_exp{m}") for m in range(2)]
        s_pick = [sem(f"picked{m}") for m in range(2)]
        s_rank = [sem(f"ranks{m}") for m in range(2)]
        s_slot = [sem(f"slots{m}") for m in range(2)]
        s_sent = [sem(f"rows_sent{m}") for m in range(2)]
        s_xe = [sem(f"expert_rows{e}") for e in range(E)]
        s_xT = [sem(f"expert_rows_T{m}") for m in range(2)]
        s_xTsb = [sem(f"expert_rows_T_sbuf{m}") for m in range(2)]
        s_up = [sem(f"expert_up{m}") for m in range(2)]
        s_silu = [sem(f"expert_silu{m}") for m in range(2)]
        s_down = [sem(f"expert_down{m}") for m in range(2)]
        s_ye = [sem(f"expert_out{m}") for m in range(2)]
        s_back = [sem(f"rows_back{m}") for m in range(2)]
        s_got = [sem(f"rows_gathered{t}") for t in range(TILES)]
        s_sum = [sem(f"block_sum{m}") for m in range(2)]
        s_most = sem("fullest_expert")
        s_oorder = sem("overflow_order")
        s_oup = sem("overflow_up")
        s_osilu = sem("overflow_silu")
        s_odown = sem("overflow_down")
        s_osum = sem("overflow_summed")
        s_out = sem("output_written")

        CAP = [SLOT, CAP_D]

        def tiles(b):
            return range(TB * b, TB * b + TB)

        def chunk_rows(cap, c):
            return min(P, cap - P * c)

        def overflows(eng):
            eng.wait_ge(s_most, 1)
            return eng.If(eng.value_load(mostu[0:1, 0:1], min_val=0, max_val=B * T) > SLOT)

        block = stack.enter_context(nc.Block())

        @block.sync
        def _(sp):
            xt = x.rearrange("b (t p) d -> p (b t) d", p=P)
            sp.dma_start(ctxs[:], ctx.rearrange("b k d -> k b d")).then_inc(s_ctx, 16)
            for b in range(B):
                sp.dma_start(xres[:, TB * b:TB * b + TB, :], xt[:, TB * b:TB * b + TB, :]).then_inc(s_x[b], 16)
            sp.dma_start(sqw[:], sq.rearrange("p (n d) -> p n d", d=D)).then_inc(s_sq, 16)
            sp.dma_start(row[:], rows.broadcast_to([P, R_END])).then_inc(s_rows, 16)
            sp.dma_start(router[:, 0, :], wg).then_inc(s_rows, 16)
            sp.dma_start(router[:, 1, :], wr).then_inc(s_rows, 16)

            def blanks(m):
                for e in range(E):
                    sp.dma_start(sent[m][e * SLOT:(e + 1) * SLOT, :].rearrange("(c p) d -> p c d", p=P),
                                 blank[:]).then_inc(s_blank[m], 16)
                for n in range(TILES):
                    sp.dma_start(back[m][n * GQ:(n + 1) * GQ, :].rearrange("(c p) d -> p c d", p=P),
                                 blank[:, 0:K2, 0:D]).then_inc(s_blank[m], 16)

            sp.wait_ge(s_set, 2)
            blanks(0)
            sp.dma_start(w1[:], w1b.rearrange("p (e f) -> p e f", e=E)).then_inc(s_w[0], 16)
            sp.dma_start(w2[:], w2b.rearrange("p (e c d) -> p e c d", e=E, c=FC)).then_inc(s_w[0], 16)
            blanks(1)
            for m in range(2):
                sp.wait_ge(s_sent[m], 16 * NPAIR // P)
                for e in range(E):
                    if m == 1:
                        sp.wait_ge(s_pair[0], e + 1)
                        sp.wait_ge(s_xT[0], e + 1)
                    sp.dma_start(xe[:, e, :, :], sent[m][e * SLOT:(e + 1) * SLOT, :]
                                 .rearrange("(c p) d -> p c d", p=P)).then_inc(s_xe[e], 16)
                sp.wait_ge(s_back[m], 16 * E * SC)
                for g in range(GROUPS):
                    if m == 1:
                        sp.wait_ge(s_sum[0], GT * (g + 1))
                    sp.dma_start(got[:, GT * g:GT * g + GT, :, :],
                                 back[m][g * GQ * K2:(g + 1) * GQ * K2, :].rearrange("(t p k) d -> p t k d", p=P, k=K2))\
                      .then_inc(s_got[g], 16)
                if m == 0:
                    sp.wait_ge(s_down[0], E)
                    sp.wait_ge(s_sum[0], 1)
                    sp.dma_start(w1[:], w1d.rearrange("p (e f) -> p e f", e=E)).then_inc(s_w[1], 16)
                    sp.dma_start(w2[:], w2d.rearrange("p (e c d) -> p e c d", e=E, c=FC)).then_inc(s_w[1], 16)
            ot = out.rearrange("b (t p) d -> p (b t) d", p=P)
            for g in range(GROUPS):
                sp.wait_ge(s_sum[1], GT * (g + 1))
                sp.dma_start(ot[:, GT * g:GT * g + GT, :], xres[:, GT * g:GT * g + GT, :]).then_inc(s_out, 16)
            sp.wait_ge(s_out, 16 * GROUPS)

        @block.gpsimd
        def _(pool):
            pool.memset(power[:], -0.5).then_inc(s_iset, 1)
            pool.memset(ident[:], 0.0).then_inc(s_iset, 1)
            pool.memset(tri[:], 1.0).then_inc(s_iset, 1)
            pool.memset(ones[:], 1.0).then_inc(s_iset, 1)
            pool.memset(onepad[:], 0.0).then_inc(s_iset, 1)
            pool.memset(vpad[:], 0.0).then_inc(s_iset, 1)
            pool.memset(blank[:, :, 0:D], 0.0).then_inc(s_set, 1)
            pool.memset(blank[:, :, D:ROW], float(NPAIR)).then_inc(s_set, 1)
            pool.wait_ge(s_iset, 6)
            pool.affine_select(out=ident[:], in_=ident[:], compare_op=ALU.not_equal, fill=1.0, base=0,
                               pattern=[[-1, P]], channel_multiplier=1).then_inc(s_set, 1)

            step = [0]

            def link(ins):
                step[0] += 1
                ins.then_inc(s_pool, 1)
                pool.wait_ge(s_pool, step[0])

            count = [0]

            def deviations(var, parts=P):
                count[0] += 1
                pool.wait_ge(s_var, count[0])
                link(pool.tensor_scalar_add(vare[0:parts, var], mv[0:parts, var, 1], EPS))
                pool.tensor_tensor(rstd[0:parts, var], vare[0:parts, var], power[0:parts, var],
                                   ALU.pow).then_inc(s_rstd, 1)

            def of_batch(b):
                return slice(TB * b, TB * b + TB)

            def of_group(g):
                return slice(GT * g, GT * g + GT)

            def send(m, g):
                pool.wait_ge(s_slot[m], g + 1)
                pool.wait_ge(s_hidk[m], g + 1)
                if g == 0:
                    pool.wait_ge(s_blank[m], 16 * (E + TILES))
                for t in range(GT * g, GT * g + GT):
                    for k in range(K2):
                        pool.indirect_dma_start(
                            sent[m], bass.IndirectOffsetOnAxis(ap=slotu[:, t, k:k + 1], axis=0),
                            hidk[:, t, k, :], None, bounds_check=NSLOT - 1, oob_is_err=False).then_inc(s_sent[m], 16)

            def second_copy(m, g):
                pool.wait_ge(s_hid[m], g + 1)
                if m == 1:
                    pool.tensor_tensor(base[:, of_group(g), :], xres[:, of_group(g), :], hidk[:, of_group(g), 0, 0:D],
                                       ALU.add).then_inc(s_base, 1)
                pool.tensor_copy(hidk[:, of_group(g), 1, 0:D], hidk[:, of_group(g), 0, 0:D]).then_inc(s_hidk[m], 1)

            def route(m):
                for g in range(GROUPS):
                    if m == 1 and g == 0:
                        pool.wait_ge(s_sent[0], 16 * NPAIR // P)
                    deviations(of_group(g))
                    if g >= 1:
                        send(m, g - 1)
                    second_copy(m, g)
                send(m, GROUPS - 1)

            def give_back(m):
                for e in range(E):
                    pool.wait_ge(s_xe[e], 16 * (m + 1))
                    if m == 1:
                        pool.wait_ge(s_back[0], 16 * E * SC)
                    pool.tensor_copy(pairu[:, e, :], xe[:, e, :, D]).then_inc(s_pair[m], 1)
                for e in range(E):
                    pool.wait_ge(s_pair[m], e + 1)
                    pool.wait_ge(s_ye[m], e + 1)
                    for c in range(SC):
                        n = chunk_rows(CAP[m], c)
                        pool.indirect_dma_start(
                            back[m], bass.IndirectOffsetOnAxis(ap=pairu[0:n, e, c:c + 1], axis=0),
                            ye[0:n, e, c, :], None, bounds_check=NPAIR - 1, oob_is_err=False).then_inc(s_back[m], 16)

            def rotary_sum(g):
                pool.wait_ge(s_rope, g + 1)
                b, at = divmod(g, GROUPS // B)
                q = qT[:, b, GQ * at:GQ * at + GQ]
                pool.tensor_tensor(q, q, ropeb[:, g % 2, :], ALU.add).then_inc(s_qsb, 1)

            deviations(slice(0, B), KV)
            for b in range(B):
                deviations(of_batch(b))
            pool.affine_select(out=tri[:], in_=tri[:], compare_op=ALU.is_gt, fill=0.0, base=0,
                               pattern=[[1, P]], channel_multiplier=-1).then_inc(s_set, 1)
            for j in range(4):
                pool.memset(onepad[:, j, DH * j:DH * j + DH], 1.0).then_inc(s_set, 1)
            for b in range(B):
                deviations(of_batch(b))
            for g in range(GROUPS):
                rotary_sum(g)
            pool.wait_ge(s_rows, 48)
            for b in range(B):
                s = of_batch(b)
                pool.tensor_tensor(base[:, s, :], xres[:, s, :], hid[:, s, :], ALU.add).then_inc(s_hbase, 1)
                pool.tensor_tensor(hidb[:, s, :], hid[:, s, :],
                                   row[:, R_BOUT:R_BOUT + D].unsqueeze(1).broadcast_to([P, TB, D]),
                                   ALU.subtract).then_inc(s_hbase, 1)
            pool.tensor_copy(hidk[:, :, :, D], cst[:, C_PAIR:C_PAIR + TILES * K2].rearrange("p (t k) -> p t k", k=K2))\
                .then_inc(s_pool, 1)
            step[0] += 1
            pool.wait_ge(s_pool, step[0])
            route(0)
            give_back(0)
            for g in range(GROUPS):
                deviations(of_group(g))
            route(1)
            give_back(1)

        @block.scalar
        def _(act):
            act.dma_start(col[:], cols).then_inc(s_cst, 16)
            act.dma_start(cst[:], consts).then_inc(s_cst, 16)

            def attention(a, u):
                if u < UNITS:
                    act.wait_ge(s_shift[a], u + 1)
                    if u >= 2:
                        act.wait_ge(s_pt[a], 2 * (u - 1))
                    act.activation(probs[:, u % 2], shifted[:, u % 2], ACT.Exp).then_inc(s_exp[a], 1)
                if 1 <= u <= UNITS:
                    v = u - 1
                    t, half = v // 2, v % 2
                    g = t // GT
                    if g >= 2 and v % UG == 0:
                        act.wait_ge(s_pv[a], g - 1)
                    for i in range(2):
                        act.wait_ge(s_pt[a], 2 * v + i + 1)
                        h0 = HALF * half + HB * i
                        act.copy(probT[0:KV, g % 2, h0:h0 + HB, P * (t % GT):P * (t % GT) + P],
                                 ps[0:KV, BT + i, :].rearrange("p (h q) -> p h q", h=HB)).then_inc(s_ptsb[a], 1)

            def tanh(a, g):
                act.wait_ge(s_zsb, g + 1)
                act.activation(norm[:, GT * g:GT * g + GT, :], ztok[:], ACT.Tanh, scale=0.5).then_inc(s_tanh, 1)

            def turned(m, g):
                act.wait_ge(s_hTp[m], g + 1)
                b, at = divmod(g, GROUPS // B)
                act.copy(inT[:, b, GQ * at:GQ * at + GQ], ps[:, BR, 0:GQ]).then_inc(s_hTsb[m], 1)

            def weights(m, g):
                act.wait_ge(s_dif[m], g + 1)
                act.activation(wexp[:, GT * g:GT * g + GT], wdif[:, GT * g:GT * g + GT], ACT.Exp).then_inc(s_wexp[m], 1)

            steps = dict(tanh=tanh, turned=turned, weights=weights)

            def experts(m):
                for e in range(E):
                    for f in range(FC):
                        n = FC * e + f
                        act.wait_ge(s_up[m], n + 1)
                        if e >= 2:
                            act.wait_ge(s_down[m], e - 1)
                        bias = col[:, V_B1 + n:V_B1 + n + 1] if m == 0 else 0.0
                        act.activation(hT[:, e % 2, f, 0:CAP[m]], ps[:, 2 + n % 4, 0:CAP[m]], ACT.Silu,
                                       bias=bias).then_inc(s_silu[m], 1)

            def attention_input(a, g):
                act.wait_ge(s_inTp, GROUPS * a + g + 1)
                b, at = divmod(g, GROUPS // B)
                dst = inT[:, b, GQ * at:GQ * at + GQ]
                if a == 0:
                    act.activation(dst, ps[:, BR, 0:GQ], ACT.Identity, scale=col[:, V_GAMMA:V_GAMMA + 1],
                                   bias=col[:, V_BETA:V_BETA + 1]).then_inc(s_inT, 1)
                else:
                    act.copy(dst, ps[:, BR, 0:GQ]).then_inc(s_inT, 1)
                    act.wait_ge(s_q, GROUPS + g + 1)
                    act.activation(qT[:, b, GQ * at:GQ * at + GQ], ps[:, BA, 0:GQ], ACT.Identity,
                                   bias=col[:, V_BQ:V_BQ + 1]).then_inc(s_qsb, 1)

            act.wait_ge(s_cst, 32)
            for a in range(2):
                for g in range(GROUPS):
                    attention_input(a, g)
                for u in range(UNITS + max(ACT_STEPS[a].values())):
                    attention(a, u)
                    for name, g in due(ACT_STEPS[a], u):
                        steps[name](a, g)
                experts(a)
                if a == 0:
                    with overflows(act):
                        for e in range(E):
                            for b in range(B):
                                n = B * e + b
                                for f in range(FC):
                                    act.wait_ge(s_oup, FC * n + f + 1)
                                    if f == 0 and n >= 1:
                                        act.wait_ge(s_odown, n)
                                    act.activation(overh[:, f, :], ps[:, f, :], ACT.Silu,
                                                   bias=col[:, V_B1 + FC * e + f:V_B1 + FC * e + f + 1])\
                                       .then_inc(s_osilu, 1)

        @block.vector
        def _(dve):
            order = {s_dve: 0, s_oorder: 0}

            def link(ins, on=s_dve):
                order[on] += 1
                ins.then_inc(on, 1)
                dve.wait_ge(on, order[on])

            def variances(src, n, at, parts=P):
                for k in range(n):
                    last = dve.bn_stats(stats[0:parts, at + k, :], src[:, k, :])
                link(last)
                for k in range(n):
                    last = dve.bn_aggr(mv[0:parts, at + k, :], stats[0:parts, at + k, :])
                last.then_inc(s_var, 1)

            group = [0]

            def normed(dst, src, n, at, parts=P):
                group[0] += 1
                dve.wait_ge(s_rstd, group[0])
                for k in range(n):
                    last = dve.tensor_scalar(dst[:, k, :], src[:, k, :], mv[0:parts, at + k, 0:1],
                                             rstd[0:parts, at + k:at + k + 1], ALU.subtract, ALU.mult)
                return last

            def attention(a, u):
                t = (u // 2) % TB
                s = ps[:, 2 * (u % 2):2 * (u % 2) + 2, 0:HB * KV].rearrange("p i (h k) -> p i h k", h=HB)
                dst = shifted[:, u % 2]
                dve.wait_ge(s_sc[a], u + 1)
                if u >= 2:
                    dve.wait_ge(s_exp[a], u - 1)
                if a == 0:
                    bias = cst[:, C_BIAS + t * KV:C_BIAS + (t + 1) * KV]
                    for i in range(2):
                        last = dve.tensor_tensor(dst[:, i], s[:, i], bias.unsqueeze(1).broadcast_to([P, HB, KV]), ALU.add)
                    last.then_inc(s_scfree[0], 1)
                    dve.wait_ge(s_scfree[0], u + 1)
                    s = dst
                link(dve.tensor_reduce(peak[:, u % 2], s, AX.X, ALU.max))
                last = dve.tensor_tensor(dst, s, peak[:, u % 2].unsqueeze(3).broadcast_to([P, 2, HB, KV]),
                                         ALU.subtract)
                last.then_inc(s_shift[a], 1)

            def rows_of(g):
                return slice(GT * g, GT * g + GT)

            def attended(a, g):
                dve.wait_ge(s_pv[a], g + 1)
                b, at = divmod(g, GROUPS // B)
                link(dve.reciprocal(rden[:], ps[:, BA, GQ:2 * GQ]))
                dve.tensor_tensor(attT[:, b, GQ * at:GQ * at + GQ], ps[:, BA, 0:GQ], rden[:], ALU.mult)\
                   .then_inc(s_att[a], 1)

            def projected(a, g):
                dve.wait_ge(s_yz, g + 1)
                dve.tensor_scalar(yT[:], ps[:, BA, 0:GQ], col[:, V_BOUT:V_BOUT + 1], None, ALU.add).then_inc(s_yT, 1)
                if g == 0:
                    dve.wait_ge(s_hbase, 2 * B)
                dve.tensor_tensor(ytok[:, rows_of(g), :], ps[:, BA, GQ:2 * GQ].rearrange("p (t d) -> p t d", t=GT),
                                  hidb[:, rows_of(g), :], ALU.subtract).then_inc(s_yzfree, 1)

            def gate(a, g):
                dve.wait_ge(s_z, g + 1)
                bgate = row[:, R_BGATE:R_BGATE + D].unsqueeze(1).broadcast_to([P, GT, D])
                dve.tensor_tensor(ztok[:], ps[:, BA, 0:GQ].rearrange("p (t d) -> p t d", t=GT), bgate, ALU.add)\
                   .then_inc(s_zsb, 1)

            def residual(a, g):
                s = rows_of(g)
                if a == 0:
                    dve.wait_ge(s_tanh, g + 1)
                    dve.wait_ge(s_yzfree, g + 1)
                    link(dve.scalar_tensor_tensor(out=ytok[:, s, :], in0=norm[:, s, :], scalar=1.0, in1=ytok[:, s, :],
                                                  op0=ALU.add, op1=ALU.mult))
                    link(dve.scalar_tensor_tensor(out=xres[:, s, :], in0=ytok[:, s, :], scalar=0.5, in1=base[:, s, :],
                                                  op0=ALU.mult, op1=ALU.add))
                else:
                    dve.wait_ge(s_yz, GROUPS + g + 1)
                    bo = row[:, R_BO:R_BO + D].unsqueeze(1).broadcast_to([P, GT, D])
                    dve.tensor_tensor(ytok[:, s, :], ps[:, BA, 0:GQ].rearrange("p (t d) -> p t d", t=GT), bo, ALU.add)\
                       .then_inc(s_yzfree, 1)
                    dve.wait_ge(s_yzfree, GROUPS + g + 1)
                    link(dve.tensor_tensor(xres[:, s, :], xres[:, s, :], ytok[:, s, :], ALU.add))
                variances(xres[:, s, :], GT, GT * g)

            def hidden(m, g):
                if m == 1 and g == 0:
                    dve.wait_ge(s_sent[0], 16 * NPAIR // P)
                normed(hidk[:, rows_of(g), 0, 0:D], xres[:, rows_of(g), :], GT, GT * g).then_inc(s_hid[m], 1)

            def choose(m, g):
                s = rows_of(g)
                dve.wait_ge(s_log[m], g + 1)
                lp = ps[:, BR, 0:GT * E].rearrange("p (t e) -> p t e", t=GT)
                if m == 0:
                    bg = row[:, R_BG:R_BG + E].unsqueeze(1).broadcast_to([P, GT, E])
                    link(dve.tensor_tensor(logit[:, s, :], lp, bg, ALU.add))
                    link(dve.tensor_scalar(logit[:, s, :], logit[:, s, :], GATE_DIV, None, ALU.mult))
                else:
                    link(dve.tensor_copy(logit[:, s, :], lp))
                for t in range(GT * g, GT * g + GT):
                    last = dve.max(top[:, t, :], logit[:, t, :])
                link(last)
                for t in range(GT * g, GT * g + GT):
                    last = dve.max_index(topi[:, t, :], top[:, t, :], logit[:, t, :])
                order[s_dve] += 1
                last.then_inc(s_dve, 1)
                dve.tensor_tensor(wdif[:, s], top[:, s, 1], top[:, s, 0], ALU.subtract).then_inc(s_dif[m], 1)
                dve.wait_ge(s_dve, order[s_dve])
                link(dve.tensor_copy(topf[:, s, :], topi[:, s, 0:K2]))
                iota = cst[:, C_IOTA:C_IOTA + E].unsqueeze(1).unsqueeze(1).broadcast_to([P, GT, K2, E])
                link(dve.tensor_tensor(pick[:, s], topf[:, s, :].unsqueeze(3).broadcast_to([P, GT, K2, E]), iota,
                                       ALU.is_equal))
                dve.tensor_tensor(picked[:, s, :], pick[:, s, 0, :], pick[:, s, 1, :], ALU.add).then_inc(s_pick[m], 1)

            def slots(m, g):
                s = rows_of(g)
                dve.wait_ge(s_rank[m], g + 1)
                rp = ps[:, BR, P:P + GT * E].rearrange("p (t e) -> p t e", t=GT)
                link(dve.tensor_tensor(ranked[:, s], pick[:, s], rp.unsqueeze(2).broadcast_to([P, GT, K2, E]), ALU.mult))
                link(dve.tensor_reduce(rank[:, s, :], ranked[:, s], AX.X, ALU.add))
                link(dve.tensor_scalar(over[:, s, :], rank[:, s, :], float(CAP[m]), float(NSLOT), ALU.is_ge, ALU.mult))
                link(dve.scalar_tensor_tensor(out=slot[:, s, :], in0=topf[:, s, :], scalar=float(SLOT),
                                              in1=rank[:, s, :], op0=ALU.mult, op1=ALU.add))
                link(dve.tensor_tensor(slot[:, s, :], slot[:, s, :], over[:, s, :], ALU.add))
                dve.tensor_scalar(slotu[:, s, :], slot[:, s, :], float(NSLOT), None, ALU.min).then_inc(s_slot[m], 1)
                dve.wait_ge(s_wexp[m], g + 1)
                link(dve.tensor_scalar(wden[:, s], wexp[:, s], 1.0, None, ALU.add))
                link(dve.reciprocal(wtok[:, s, 0], wden[:, s]))
                link(dve.tensor_tensor(wtok[:, s, 1], wexp[:, s], wtok[:, s, 0], ALU.mult))
                if m == 0 and g == GROUPS - 1:
                    link(dve.tensor_reduce(most[:], ps[:, BR, 2 * P:2 * P + E], AX.X, ALU.max))
                    dve.tensor_copy(mostu[:], most[:]).then_inc(s_most, 1)

            steps = dict(attended=attended, projected=projected, gate=gate, residual=residual, hidden=hidden,
                         choose=choose, slots=slots)

            def keys_and_values(a):
                dve.wait_ge(s_kv, a + 1)
                kp = ps[:, 2, 0:B * KV].rearrange("p (b k) -> p b k", b=B)
                if a == 0:
                    kr = ps[:, 2, 256:256 + B * KV].rearrange("p (b k) -> p b k", b=B)
                    cos = cst[:, C_COS:C_COS + KV].unsqueeze(1).broadcast_to([P, B, KV])
                    sin = cst[:, C_SIN:C_SIN + KV].unsqueeze(1).broadcast_to([P, B, KV])
                    link(dve.tensor_tensor(kT[:], kp, cos, ALU.mult))
                    link(dve.tensor_tensor(ropek[:], kr, sin, ALU.mult))
                    link(dve.tensor_tensor(kT[:], kT[:], ropek[:], ALU.add))
                else:
                    link(dve.tensor_scalar(kT[:], kp, col[:, V_BK:V_BK + 1], None, ALU.add))
                if a == 0:
                    dve.wait_ge(s_iset, 6)
                for b in range(B):
                    v = ps[0:KV, 3, b * D:(b + 1) * D].rearrange("p (g j d) -> p g j d", g=4, j=4)
                    for j in range(4):
                        dst = vpad[:, b, j:H:4, DH * j:DH * j + DH]
                        if a == 0:
                            last = dve.tensor_copy(dst, v[:, :, j, :])
                        else:
                            bv = row[0:KV, R_BV:R_BV + D].rearrange("p (g j d) -> p g j d", g=4, j=4)
                            last = dve.tensor_tensor(dst, v[:, :, j, :], bv[:, :, j, :], ALU.add)
                last.then_inc(s_kvfree, 1)
                mask = cst[:, C_MASK:C_MASK + H].unsqueeze(2).broadcast_to([P, H, KV])
                for b in range(B):
                    last = dve.tensor_tensor(kbd[:, b], kT[:, b, :].unsqueeze(1).broadcast_to([P, H, KV]), mask, ALU.mult)
                    last.then_inc(s_kvsb, 1)

            def queries(g):
                b, at = divmod(g, GROUPS // B)
                s = slice(GQ * at, GQ * at + GQ)
                dve.wait_ge(s_q, g + 1)
                if g >= 2:
                    dve.wait_ge(s_qsb, g - 1)
                dve.tensor_tensor(qT[:, b, s], ps[:, BA, 0:GQ], cst[:, C_COS + GQ * at:C_COS + GQ * at + GQ], ALU.mult)
                dve.tensor_tensor(ropeb[:, g % 2, :], ps[:, BA, GQ:2 * GQ],
                                  cst[:, C_SIN + GQ * at:C_SIN + GQ * at + GQ], ALU.mult).then_inc(s_rope, 1)

            def experts(m):
                for e in range(E + 1):
                    if e < E:
                        dve.wait_ge(s_xT[m], e + 1)
                        if e >= 2:
                            dve.wait_ge(s_up[m], FC * (e - 1))
                        dve.tensor_copy(xeT[:, e % 2, 0:CAP[m]], ps[:, e % 2, 0:CAP[m]]).then_inc(s_xTsb[m], 1)
                    if e >= 1:
                        o = e - 1
                        dve.wait_ge(s_down[m], o + 1)
                        if m == 1 and o == 0:
                            dve.wait_ge(s_back[0], 16 * E * SC)
                        for c in range(SC):
                            n = chunk_rows(CAP[m], c)
                            src = ps[0:n, 6 + o % 2, c * P:(c + 1) * P]
                            if m == 0:
                                last = dve.tensor_tensor(ye[0:n, o, c, :], src,
                                                         row[0:n, R_B2 + o * D:R_B2 + (o + 1) * D], ALU.add)
                            else:
                                last = dve.tensor_copy(ye[0:n, o, c, :], src)
                        last.then_inc(s_ye[m], 1)

            def combine(m, g):
                src = xres if m == 0 else base
                dve.wait_ge(s_got[g], 16 * (m + 1))
                if m == 1:
                    dve.wait_ge(s_base, g + 1)
                tiles = range(GT * g, GT * g + GT)
                for t in tiles:
                    last = dve.scalar_tensor_tensor(out=norm[:, t, :], in0=got[:, t, 0, :], scalar=wtok[:, t, 0:1],
                                                    in1=src[:, t, :], op0=ALU.mult, op1=ALU.add)
                link(last)
                for t in tiles:
                    dve.scalar_tensor_tensor(out=xres[:, t, :], in0=got[:, t, 1, :], scalar=wtok[:, t, 1:2],
                                             in1=norm[:, t, :], op0=ALU.mult, op1=ALU.add).then_inc(s_sum[m], 1)

            def before_attention(g):
                combine(0, g)
                dve.wait_ge(s_sum[0], GT * (g + 1))
                variances(xres[:, rows_of(g), :], GT, GT * g)

            def attention_norm(g):
                normed(norm[:, rows_of(g), :], xres[:, rows_of(g), :], GT, GT * g).then_inc(s_norm, 1)

            dve.wait_ge(s_ctx, 16)
            variances(ctxs[:], B, 0, KV)
            normed(ctxn[:], ctxs[:], B, 0, KV).then_inc(s_ctxn, 1)
            dve.wait_ge(s_ctxn, 1)
            for b in range(B):
                dve.wait_ge(s_x[b], 16)
                variances(xres[:, TB * b:TB * b + TB, :], TB, TB * b)
            for b in range(B):
                s = slice(TB * b, TB * b + TB)
                normed(hid[:, s, :], xres[:, s, :], TB, TB * b).then_inc(s_h, 1)
                dve.wait_ge(s_h, b + 1)
                variances(hid[:, s, :], TB, TB * b)
            dve.wait_ge(s_cst, 32)
            dve.wait_ge(s_ctxT, 1)
            dve.tensor_scalar(kinT[:], ps[:, 0, 0:B * KV].rearrange("p (b k) -> p b k", b=B),
                              col[:, V_GAMMA:V_GAMMA + 1], col[:, V_BETA:V_BETA + 1], ALU.mult, ALU.add)\
               .then_inc(s_kin, 1)
            for b in range(B):
                s = slice(TB * b, TB * b + TB)
                normed(norm[:, s, :], hid[:, s, :], TB, TB * b).then_inc(s_norm, 1)
                if b == 0:
                    keys_and_values(0)
            for g in range(GROUPS):
                queries(g)
            dve.wait_ge(s_rows, 48)
            for u in range(UNITS + max(DVE_STEPS[0].values())):
                if u < UNITS:
                    attention(0, u)
                for name, g in due(DVE_STEPS[0], u):
                    steps[name](0, g)
            dve.wait_ge(s_ctxT, 2)
            dve.tensor_copy(kinT[:], ps[:, 0, 0:B * KV].rearrange("p (b k) -> p b k", b=B)).then_inc(s_kin, 1)
            keys_and_values(1)
            experts(0)
            with overflows(dve):
                link(dve.tensor_tensor(ranked[:], pick[:], over[:].unsqueeze(3).broadcast_to([P, TILES, K2, E]),
                                       ALU.mult), s_oorder)
                link(dve.tensor_tensor(ranked[:], ranked[:], wtok[:].unsqueeze(3).broadcast_to([P, TILES, K2, E]),
                                       ALU.mult), s_oorder)
                link(dve.tensor_tensor(wover[:], ranked[:, :, 0, :], ranked[:, :, 1, :], ALU.add), s_oorder)
                link(dve.tensor_scalar(wover[:], wover[:], 1.0 / NSLOT, None, ALU.mult), s_oorder)
                for e in range(E):
                    b2 = row[:, R_B2 + e * D:R_B2 + (e + 1) * D].unsqueeze(1).broadcast_to([P, TB, D])
                    for b in range(B):
                        dve.wait_ge(s_odown, B * e + b + 1)
                        y = ytok[:, 0:TB, :]
                        dve.tensor_tensor(y, ps[:, 4, :].rearrange("p (t d) -> p t d", t=TB), b2, ALU.add)\
                           .then_inc(s_osum, 1)
                        dve.wait_ge(s_osum, B * e + b + 1)
                        for k in range(TB):
                            t = TB * b + k
                            last = dve.scalar_tensor_tensor(out=xres[:, t, :], in0=y[:, k, :], scalar=wover[:, t, e:e + 1],
                                                            in1=xres[:, t, :], op0=ALU.mult, op1=ALU.add)
                        link(last, s_oorder)
            for g in range(GROUPS + 1):
                if g < GROUPS:
                    before_attention(g)
                if g >= 1:
                    attention_norm(g - 1)
            for u in range(UNITS + max(DVE_STEPS[1].values())):
                if u < UNITS:
                    attention(1, u)
                for name, g in due(DVE_STEPS[1], u):
                    steps[name](1, g)
            experts(1)
            for g in range(GROUPS):
                combine(1, g)

        @block.tensor
        def _(pe):
            def transposed(bank, src, n, parts=P):
                for k in range(n):
                    last = pe.matmul(ps[:, bank, k * parts:(k + 1) * parts], src(k), ident[0:parts, 0:parts],
                                     start=True, stop=True, is_transpose=True)
                return last

            def scores(a, u):
                b, t = u // UB, (u // 2) % TB
                if u % UG == 0:
                    pe.wait_ge(s_qsb, GROUPS * a + u // UG + 1)
                if u % UB == 0:
                    pe.wait_ge(s_kvsb, B * a + b + 1)
                if u >= 2:
                    pe.wait_ge(s_scfree[0] if a == 0 else s_shift[1], u - 1)
                for i in range(2):
                    h0 = HALF * (u % 2) + HB * i
                    last = pe.matmul(ps[:, 2 * (u % 2) + i, 0:HB * KV], qT[:, b, t * P:(t + 1) * P],
                                     kbd[:, b, h0:h0 + HB, :].rearrange("p h k -> p (h k)"), start=True, stop=True)
                last.then_inc(s_sc[a], 1)

            def transpose_probs(a, u):
                pe.wait_ge(s_exp[a], u + 1)
                for i in range(2):
                    if u >= 1:
                        pe.wait_ge(s_ptsb[a], 2 * (u - 1) + i + 1)
                    for h in range(HB):
                        last = pe.matmul(ps[0:KV, BT + i, h * P:(h + 1) * P], probs[:, u % 2, i, h, :], ident[:],
                                         start=True, stop=True, is_transpose=True)
                    last.then_inc(s_pt[a], 1)

            def attend(a, g):
                b = g // (GROUPS // B)
                pe.wait_ge(s_ptsb[a], 2 * UG * (g + 1))
                if g >= 1:
                    pe.wait_ge(s_zsb if a == 0 else s_yzfree, g if a == 0 else GROUPS + g)
                for at, weights in ((0, vpad[:, b]), (GQ, None)):
                    for j in range(4):
                        for q in range(4):
                            h = 4 * q + j
                            w = onepad[:, j, :] if weights is None else vpad[:, b, h, :]
                            last = pe.matmul(ps[32 * q:32 * q + 32, BA, at:at + GQ], w, probT[0:KV, g % 2, h, :],
                                             start=(j == 0), stop=(j == 3))
                last.then_inc(s_pv[a], 1)

            def project(a, g):
                pe.wait_ge(s_att[a], g + 1)
                b, at = divmod(g, GROUPS // B)
                q0 = GQ * at
                if a == 0:
                    pe.matmul(ps[:, BA, 0:GQ], weight("out0"), attT[:, b, q0:q0 + GQ], start=True, stop=True)
                for k in range(GT):
                    o = (GQ if a == 0 else 0) + k * D
                    last = pe.matmul(ps[:, BA, o:o + D], attT[:, b, q0 + k * P:q0 + (k + 1) * P],
                                     weight("out0" if a == 0 else "o1"), start=True, stop=True)
                last.then_inc(s_yz, 1)

            def gate(a, g):
                pe.wait_ge(s_yT, g + 1)
                pe.wait_ge(s_yzfree, g + 1)
                for k in range(GT):
                    last = pe.matmul(ps[:, BA, k * D:(k + 1) * D], yT[:, k * P:(k + 1) * P], weight("gate0"),
                                     start=True, stop=True)
                last.then_inc(s_z, 1)

            def turn(m, g):
                pe.wait_ge(s_hid[m], g + 1)
                if g >= 1:
                    pe.wait_ge(s_slot[m], g)
                if m == 1 and g == 0:
                    pe.wait_ge(s_inT, 2 * GROUPS)
                transposed(BR, lambda k: hidk[:, GT * g + k, 0, 0:D], GT).then_inc(s_hTp[m], 1)

            def logits(m, g):
                pe.wait_ge(s_hTsb[m], g + 1)
                b, at = divmod(g, GROUPS // B)
                for k in range(GT):
                    q0 = GQ * at + k * P
                    last = pe.matmul(ps[:, BR, k * E:(k + 1) * E], inT[:, b, q0:q0 + P], router[:, m, :],
                                     start=True, stop=True)
                last.then_inc(s_log[m], 1)

            def ranks(m, g):
                pe.wait_ge(s_pick[m], g + 1)
                for k in range(GT):
                    t = GT * g + k
                    for s in range(t + 1):
                        last = pe.matmul(ps[:, BR, P + k * E:P + (k + 1) * E], tri[:] if s == t else ones[:],
                                         picked[:, s, :], start=(s == 0), stop=(s == t))
                if m == 0 and g == GROUPS - 1:
                    for t in range(TILES):
                        last = pe.matmul(ps[:, BR, 2 * P:2 * P + E], ones[:], picked[:, t, :],
                                         start=(t == 0), stop=(t == TILES - 1))
                last.then_inc(s_rank[m], 1)

            steps = dict(attend=attend, project=project, gate=gate, turn=turn, logits=logits, ranks=ranks)

            def attention(a):
                scores(a, 0)
                scores(a, 1)
                for u in range(UNITS + max(PE_STEPS[a].values())):
                    if u + 2 < UNITS:
                        scores(a, u + 2)
                    if u < UNITS:
                        transpose_probs(a, u)
                    for name, g in due(PE_STEPS[a], u):
                        steps[name](a, g)

            def experts(m):
                cap = CAP[m]
                pe.wait_ge(s_w[m], 32)
                pe.wait_ge(s_slot[m], GROUPS)
                if m == 0:
                    pe.wait_ge(s_most, 1)
                    pe.wait_ge(s_kvfree, 2)

                def rows_in(e):
                    pe.wait_ge(s_xe[e], 16 * (m + 1))
                    if e >= 2:
                        pe.wait_ge(s_xTsb[m], e - 1)
                    for c in range(SC):
                        n = chunk_rows(cap, c)
                        last = pe.matmul(ps[:, e % 2, c * P:c * P + n], xe[0:n, e, c, 0:D], ident[0:n, 0:n],
                                         start=True, stop=True, is_transpose=True)
                    last.then_inc(s_xT[m], 1)

                def up(e):
                    pe.wait_ge(s_xTsb[m], e + 1)
                    for f in range(FC):
                        n = FC * e + f
                        if n >= 4:
                            pe.wait_ge(s_silu[m], n - 3)
                        pe.matmul(ps[:, 2 + n % 4, 0:cap], w1[:, e, f * P:(f + 1) * P], xeT[:, e % 2, 0:cap],
                                  start=True, stop=True).then_inc(s_up[m], 1)

                def down(e):
                    pe.wait_ge(s_silu[m], FC * (e + 1))
                    if e >= 2:
                        pe.wait_ge(s_ye[m], e - 1)
                    for c in range(SC):
                        n = chunk_rows(cap, c)
                        for f in range(FC):
                            last = pe.matmul(ps[0:n, 6 + e % 2, c * P:(c + 1) * P], hT[:, e % 2, f, c * P:c * P + n],
                                             w2[:, e, f, :], start=(f == 0), stop=(f == FC - 1))
                    last.then_inc(s_down[m], 1)

                rows_in(0)
                for e in range(E + 1):
                    if e + 1 < E:
                        rows_in(e + 1)
                    if e < E:
                        up(e)
                    if e >= 1:
                        down(e - 1)

            def project_kv(a):
                pe.wait_ge(s_kin, a + 1)
                names = (("k0", 0), ("k0p", 256)) if a == 0 else (("k1", 0),)
                for name, at in names:
                    pe.matmul(ps[:, 2, at:at + B * KV], weight(name), kinT[:].rearrange("p b k -> p (b k)"),
                              start=True, stop=True)
                for b in range(B):
                    last = pe.matmul(ps[0:KV, 3, b * D:(b + 1) * D], kinT[:, b, :], weight(f"v{a}"),
                                     start=True, stop=True)
                last.then_inc(s_kv, 1)

            def project_q(a, g):
                b, at = divmod(g, GROUPS // B)
                q = inT[:, b, GQ * at:GQ * at + GQ]
                pe.wait_ge(s_norm, b + 1 if a == 0 else B + g + 1)
                if g >= 1:
                    pe.wait_ge(s_inT, GROUPS * a + g)
                transposed(BR, lambda k: norm[:, GT * g + k, :], GT).then_inc(s_inTp, 1)
                pe.wait_ge(s_inT, GROUPS * a + g + 1)
                if g >= 1:
                    pe.wait_ge(s_rope if a == 0 else s_qsb, g if a == 0 else GROUPS + g)
                last = pe.matmul(ps[:, BA, 0:GQ], weight(f"q{a}"), q, start=True, stop=True)
                if a == 0:
                    last = pe.matmul(ps[:, BA, GQ:2 * GQ], weight("q0p"), q, start=True, stop=True)
                last.then_inc(s_q, 1)

            pe.wait_ge(s_set, 3)
            pe.wait_ge(s_ctxn, 1)
            transposed(0, lambda k: ctxn[:, k, :], B, KV).then_inc(s_ctxT, 1)
            pe.wait_ge(s_sq, 16)
            project_kv(0)
            for g in range(GROUPS):
                project_q(0, g)
            pe.wait_ge(s_kvfree, 1)
            pe.wait_ge(s_rope, GROUPS)
            pe.wait_ge(s_set, 8)
            pe.wait_ge(s_rows, 48)
            attention(0)
            transposed(0, lambda k: ctxs[:, k, :], B, KV).then_inc(s_ctxT, 1)
            project_kv(1)
            experts(0)
            pe.wait_ge(s_ye[0], E)
            with overflows(pe):
                for e in range(E):
                    for b in range(B):
                        n = B * e + b
                        for f in range(FC):
                            if n >= 1:
                                pe.wait_ge(s_osilu, FC * (n - 1) + f + 1)
                            pe.matmul(ps[:, f, :], w1[:, e, f * P:(f + 1) * P], inT[:, b, :], start=True, stop=True)\
                              .then_inc(s_oup, 1)
                        pe.wait_ge(s_osilu, FC * (n + 1))
                        if n >= 1:
                            pe.wait_ge(s_osum, n)
                        for k in range(TB):
                            for f in range(FC):
                                last = pe.matmul(ps[:, 4, k * P:(k + 1) * P], overh[:, f, k * P:(k + 1) * P],
                                                 w2[:, e, f, :], start=(f == 0), stop=(f == FC - 1))
                        last.then_inc(s_odown, 1)
            for g in range(GROUPS):
                project_q(1, g)
            attention(1)
            experts(1)


def partner(w):
    return w.reshape(D, H, 2, DH // 2)[:, :, ::-1, :].reshape(D, D)


def kernel(x, ctx_1024, L0_xattn_Wqkv, L0_xattn_Wout, L0_xattn_b_out, L0_xattn_Wgate, L0_xattn_b_gate,
           L0_xattn_gamma, L0_xattn_beta, L0_ffn_Wg, L0_ffn_bg, L0_ffn_W1, L0_ffn_b1, L0_ffn_W2, L0_ffn_b2,
           L1_xattn_W_Q, L1_xattn_b_Q, L1_xattn_W_K, L1_xattn_b_K, L1_xattn_W_V, L1_xattn_b_V,
           L1_xattn_W_O, L1_xattn_b_O, L1_ffn_router_w, L1_ffn_w1, L1_ffn_w2):
    import concourse.bacc as bacc
    from concourse.bass_utils import run_bass_kernel_spmd

    a = {k: np.asarray(v) for k, v in locals().items() if k not in ("bacc", "run_bass_kernel_spmd")}
    wqkv = a["L0_xattn_Wqkv"]
    wq, wk, wv = wqkv[:D].T, wqkv[D:2 * D].T, wqkv[2 * D:].T
    square = [wq, partner(wq), wk, partner(wk), wv, a["L0_xattn_Wout"].T, a["L0_xattn_Wgate"].T,
              a["L1_xattn_W_Q"], a["L1_xattn_W_K"], a["L1_xattn_W_V"], a["L1_xattn_W_O"]]
    b1 = a["L0_ffn_b1"].reshape(E * FC, P).T
    cols = [a["L0_xattn_gamma"][:, None], a["L0_xattn_beta"][:, None], a["L0_xattn_b_out"][:, None],
            a["L1_xattn_b_Q"][:, None], a["L1_xattn_b_K"][:, None], b1]
    rows = [a["L0_xattn_b_out"], a["L0_xattn_b_gate"], a["L1_xattn_b_O"], a["L1_xattn_b_V"], a["L0_ffn_bg"],
            a["L0_ffn_b2"].reshape(-1)]

    def up(w):
        return w.transpose(1, 0, 2).reshape(P, E * FF)

    def down(w):
        return w.reshape(E, FC, P, D).transpose(2, 0, 1, 3).reshape(P, E * FC * D)

    arrays = {
        "x": a["x"], "ctx": a["ctx_1024"], "consts": constants(), "square": np.concatenate(square, axis=1),
        "cols": np.concatenate(cols, axis=1), "rows": np.concatenate(rows)[None, :],
        "wg": a["L0_ffn_Wg"], "wr": a["L1_ffn_router_w"].T,
        "w1b": up(a["L0_ffn_W1"]), "w2b": down(a["L0_ffn_W2"]),
        "w1d": up(a["L1_ffn_w1"]), "w2d": down(a["L1_ffn_w2"]),
    }
    arrays = {k: np.ascontiguousarray(v) for k, v in arrays.items()}
    nc = bacc.Bacc("TRN2", target_bir_lowering=False, num_devices=1)
    args = [nc.dram_tensor(k, v.shape, mybir.dt.from_np(v.dtype), kind="ExternalInput").ap() for k, v in arrays.items()]
    out = nc.dram_tensor("out", (B, T, D), mybir.dt.float32, kind="ExternalOutput").ap()
    two_block_kernel(nc, *args, out)
    r = run_bass_kernel_spmd(nc, [arrays], core_ids=[0])
    return r.results[0]["out"]
```

```python
import numpy as np
import concourse.bass as bass
from concourse import mybir
from contextlib import ExitStack

B, T, D = 2, 512, 128
KV = 77
H, DH = 16, 8
P = 128
TILES = B * T // P
TB = T // P
KP = KV + 1
Q4 = 4
BN = 128
NEAR = P * BN // T + 2
LOW = 64
ST = 3 * H // Q4 * DH
GT = 2
GROUPS = TILES // GT
GQ = GT * P
UG = H // Q4
UNITS = UG * GROUPS
AHEAD = 2
RING = 4
E, K2 = 8, 2
FF = 512
FC = FF // P
SLOT = 384
SC = SLOT // P
PIECE = 2
PIECES = E // PIECE
RAWS = 3
NSLOT = E * SLOT
NPAIR = B * T * K2
ROW = D + 1
CAP_D = int(1.25 * B * T * K2 / E) + 1
EPS = 1e-5
SCALE = DH ** -0.5
GATE_DIV = float(np.float32(1.0) / np.float32(1.0 + 1e-6))

WARM_START = 13
WARM_SUM = 12
WARM_TAIL = [0, 2]
WARM_ROWS = [3, 3]

C_COS, C_SIN, C_MASK = 0, T, 2 * T
C_IOTA = C_MASK + Q4
C_PAIR = C_IOTA + E
C_BROW = C_PAIR + TILES * K2
C_BCOL = C_BROW + TB * KP
C_END = C_BCOL + TB * P
R_BOUT, R_BGATE, R_BO, R_BV, R_BG, R_B2 = 0, D, 2 * D, 3 * D, 4 * D, 4 * D + E
R_END = R_B2 + E * D
V_GAMMA, V_BETA, V_BOUT, V_BQ, V_BK, V_B1 = 0, 1, 2, 3, 4, 5
V_END = V_B1 + E * FC
W_FIRST = 5
W_NAMES = ["q0", "q0p", "k0", "k0p", "v0", "out0", "gate0", "q1", "k1", "v1", "o1"]


PE_STEPS = [dict(gate3=5, project=4, gate=7, turn=9, logits=10, ranks=11, next_context=8, next_parts=10,
                 next_keys=11, turn3=7, logits3=9, ranks3=10),
            dict(project=4, turn=7, logits=7, ranks=9)]
DVE_STEPS = [dict(attended=5, projected3=6, residual3=7, hidden3=9, projected=8, residual=9, hidden=10,
                  choose=12, slots=13, next_context=11, next_parts=13, next_keys=14, choose3=11, slots3=12),
             dict(attended=5, residual=7, hidden=8, choose=10, slots=11)]
ACT_STEPS = [dict(projected3=4, tanh3=5, projected=5, tanh=7, copies=8, turned=9),
             dict(copies=9, turned=7)]
POOL_STEPS = [dict(deviation=10, residual=12, send=15),
              dict(deviation=5, residual=7, send=10)]
PE_QUERIES = [[(-1, "tokens", 0), (-1, "queries", 0), (-1, "keys", 0), (-1, "tokens", 1), (-1, "tokens", 2),
               (-1, "queries", 1), (-1, "stack", 0), (-1, "queries", 2), (-1, "tokens", 3), (-1, "stack", 1),
               (0, "queries", 3), (1, "stack", 2), (2, "stack", 3)],
              [(-1, "tokens", 0), (-1, "queries", 0), (-1, "tokens", 1), (-1, "tokens", 2), (-1, "queries", 1),
               (-1, "stack", 0), (-1, "tokens", 3), (-1, "queries", 2), (-1, "stack", 1), (0, "queries", 3),
               (1, "stack", 2), (2, "stack", 3)]]
ACT_QUERIES = [[(-1, "tokens", 0), (-1, "keys", 0), (-1, "tokens", 1), (-1, "high", 0), (-1, "tokens", 2),
                (-1, "high", 1), (-1, "stack", 0), (-1, "tokens", 3), (-1, "high", 2), (-1, "stack", 1),
                (0, "high", 3), (1, "stack", 2), (2, "stack", 3)],
               [(-1, "tokens", 0), (-1, "keys", 0), (-1, "high", 0), (-1, "tokens", 1), (-1, "high", 1),
                (-1, "tokens", 2), (-1, "stack", 0), (-1, "tokens", 3), (-1, "high", 2), (-1, "stack", 1),
                (0, "high", 3), (1, "stack", 2), (2, "stack", 3)]]
DVE_QUERIES = [[(-1, "rotated", 0), (-1, "keys", 0), (-1, "rotated", 1), (-1, "stack", 0), (-1, "rotated", 2),
                (-1, "bias", 0), (-1, "stack", 1), (0, "rotated", 3), (1, "stack", 2), (1, "stack", 3),
                (3, "keys", 1)],
               [(-1, "sum", 0), (-1, "sum", 1), (-1, "norm", 0), (-1, "sum", 2), (-1, "norm", 1),
                (-1, "sum", 3), (-1, "norm", 2), (-1, "norm", 3), (-1, "low", 0), (-1, "low", 1),
                (-1, "stack", 0), (-1, "low", 2), (-1, "stack", 1), (0, "low", 3), (1, "stack", 2),
                (2, "stack", 3)]]
WEIGHT_TURNS = [[6, 7, 8, 9], [3, 4, 5, 6]]


def at_turn(queries, turn):
    return [(name, g) for when, name, g in queries if when == turn]


def due(steps, u):
    for name, delay in steps.items():
        g, rest = divmod(u - delay - (UG - 1), UG)
        if name[-1] == "3":
            if u == UNITS - 1 + delay:
                yield name[:-1], GROUPS - 1
        elif rest == 0 and 0 <= g < GROUPS and not (g == GROUPS - 1 and name + "3" in steps):
            yield name, g


def bias_factors():
    pos = np.arange(BN, dtype=np.float64)
    dist = np.abs(pos[None, :] - pos[:, None])
    bias = np.exp(-dist * 0.1) - dist * 0.05

    def weights(out):
        inv = BN / out
        at = (np.arange(out) + 0.5) * inv - 0.5
        w = np.maximum(0.0, 1.0 - np.abs(at[None, :] - np.arange(BN)[:, None]) / max(inv, 1.0))
        return w / w.sum(axis=0, keepdims=True)

    over_keys = bias @ weights(KV)
    over_tokens = weights(T)
    for t in range(TB):
        first = min(max(t * P * BN // T - 1, 0), BN - NEAR)
        yield over_keys[first:first + NEAR], over_tokens[first:first + NEAR, t * P:(t + 1) * P]


def constants():
    c = np.zeros((P, C_END), np.float32)
    half = DH // 2
    inv_freq = 1.0 / 10000.0 ** (np.arange(0, DH, 2, dtype=np.float32) / np.float32(DH))
    freqs = np.arange(T, dtype=np.float32)[:, None] * inv_freq.astype(np.float32)[None, :]
    lane = np.arange(P) % DH
    angle = freqs[:, lane % half].T.astype(np.float32)
    c[:, C_COS:C_COS + T] = np.cos(angle.astype(np.float64))
    c[:, C_SIN:C_SIN + T] = np.where(lane[:, None] < half, -1.0, 1.0) * np.sin(angle.astype(np.float64))
    for t, (by_key, by_token) in enumerate(bias_factors()):
        for first in (0, LOW):
            c[first:first + NEAR, C_BROW + t * KP:C_BROW + t * KP + KV] = by_key
            c[first:first + NEAR, C_BCOL + t * P:C_BCOL + (t + 1) * P] = by_token
    part = np.arange(P)[:, None]
    own = np.where(part < ST, part // DH % Q4, part - ST)
    c[:, C_MASK:C_MASK + Q4] = own == np.arange(Q4)[None, :]
    c[:, C_IOTA:C_IOTA + E] = np.arange(E)[None, :]
    token = np.arange(TILES)[None, :, None] * P + np.arange(P)[:, None, None]
    c[:, C_PAIR:C_PAIR + TILES * K2] = (token * K2 + np.arange(K2)).reshape(P, TILES * K2)
    return c


def two_block_kernel(nc, x, ctx, consts, sq, cols, rows, wg, wr, w1b, w2b, w1d, w2d, out):
    F32, BF16, U32 = mybir.dt.float32, mybir.dt.bfloat16, mybir.dt.uint32
    F32R = mybir.dt.float32r
    ALU = mybir.AluOpType
    ACT = mybir.ActivationFunctionType
    AX = mybir.AxisListType

    with ExitStack() as stack:
        def sb(name, shape, dt=F32):
            return stack.enter_context(nc.sbuf_tensor(name, shape, dt))

        def sem(name):
            return stack.enter_context(nc.semaphore(name))

        sent = [nc.dram_tensor(f"sent{m}", (NSLOT, ROW), F32, kind="Internal").ap() for m in range(2)]
        back = [nc.dram_tensor(f"back{m}", (NPAIR, D), F32, kind="Internal").ap() for m in range(2)]

        cst = sb("cst", [P, C_END])
        sqw = sb("sqw", [P, len(W_NAMES), D])
        col = sb("col", [P, V_END])
        row = sb("row", [P, R_END])
        router = sb("router", [P, 2, E])
        w1hi = sb("w1hi", [P, E, FF], F32R)
        w1lo = sb("w1lo", [P, E, FF], F32R)
        w2 = sb("w2", [P, E, FC, D])
        blank = sb("blank", [P, SC, ROW])
        ident = sb("ident", [P, P])
        tri = sb("tri", [P, P], BF16)
        ones = sb("ones", [P, P], BF16)
        power = sb("power", [P, TILES])
        hidk = sb("hidk", [P, TILES, K2, ROW])
        hidb = sb("hidb", [P, TILES, D])
        pairu = sb("pairu", [P, E, SC], U32)
        xres = sb("xres", [P, TILES, D])
        hid = sb("hid", [P, TILES, D])
        base = sb("base", [P, TILES, D])
        norm = sb("norm", [P, TILES, D])
        ctxs = sb("ctxs", [KV, B, D])
        ctxn = sb("ctxn", [KV, B, D])
        stats = sb("stats", [P, TILES, 6])
        mv = sb("mv", [P, TILES, 2])
        vare = sb("vare", [P, TILES])
        rstd = sb("rstd", [P, TILES])
        inT = sb("inT", [P, B, T])
        kinT = sb("kinT", [P, B, KV])
        q32 = sb("q32", [P, 2, GQ])
        ropeb = sb("ropeb", [P, 2, GQ])
        qhi = sb("qhi", [P, 2, GQ], F32R)
        qlo = sb("qlo", [P, 2, GQ], F32R)
        sel = sb("sel", [P, 2, UG, ST], F32R)
        kT = sb("kT", [P, B, KP])
        ropek = sb("ropek", [P, B, KV])
        khi = sb("khi", [P, B, KP], F32R)
        klo = sb("klo", [P, B, KP], F32R)
        krep = sb("krep", [ST, UG, B * KP])
        qst = sb("qst", [P, UG, B * T], F32R)
        kst = sb("kst", [P, B, H, KP], F32R)
        vpad = sb("vpad", [KV, B, H, 32])
        onepad = sb("onepad", [KV, 4, 32])
        peak = sb("peak", [P, 2, GT, Q4])
        probT = sb("probT", [P, RING, Q4, GQ])
        bkey = sb("bkey", [P, TB, KP], F32R)
        btok = sb("btok", [P, TB, P], F32R)
        spare = sb("spare", [1, 4])
        one = sb("one", [1, P])
        attT = sb("attT", [P, B, T])
        numden = cst[:, 0:2 * GQ].rearrange("p (i t) -> p i t", i=2)
        rden = cst[:, 2 * GQ:3 * GQ]
        yT = cst[:, 3 * GQ:4 * GQ]
        ytok = hidb
        gbias = sb("gbias", [P, E])
        logit = sb("logit", [P, TILES, E])
        top = sb("top", [P, TILES, 8])
        topi = sb("topi", [P, TILES, 8], U32)
        topf = sb("topf", [P, TILES, K2])
        pick = sb("pick", [P, TILES, K2, E])
        picked = sb("picked", [P, TILES, E], BF16)
        ranked = sb("ranked", [P, TILES, K2, E])
        rank = sb("rank", [P, TILES, K2])
        slot = sb("slot", [P, TILES, K2])
        over = sb("over", [P, TILES, K2])
        slotu = sb("slotu", [P, TILES, K2], U32)
        wdif = sb("wdif", [P, TILES])
        wexp = sb("wexp", [P, TILES])
        wden = sb("wden", [P, TILES])
        wtok = sb("wtok", [P, TILES, K2])
        xe = sb("xe", [P, E, SC, ROW])
        xhi = sb("xhi", [P, 2, SLOT], F32R)
        xlo = sb("xlo", [P, 2, SLOT], F32R)
        hT = sb("hT", [P, 2, FC, SLOT])
        ye = probT[:].rearrange("p g h q -> p (g h q)")[:, 0:E * SC * D].rearrange("p (e c d) -> p e c d", e=E, c=SC)
        got = xe[:].rearrange("p e c d -> p (e c d)")[:, 0:TILES * K2 * D]\
            .rearrange("p (t k d) -> p t k d", t=TILES, k=K2)
        raw = hT[:].rearrange("p a f s -> p (a f s)").rearrange("p (n e f) -> p n e f", e=PIECE, f=FF)
        most = sb("most", [P, 1])
        mostu = sb("mostu", [P, 1], U32)
        wover = sb("wover", [P, TILES, E])
        overh = hT[:].rearrange("p a f s -> p (a f s)")[:, 0:FC * T].rearrange("p (f t) -> p f t", f=FC)

        ps = stack.enter_context(nc.psum_tensor("ps", [P, 8, 512], F32))
        BS, BK, BNUM, BDEN, BY, BR = 0, 2, 4, 5, 6, 7
        STACK_BANKS = [BS, BK, BY, BNUM]

        def tokens_bank(g):
            return (BR, BNUM)[g % 2]

        def queries_bank(g):
            return (BY, BDEN)[g % 2]

        def weight(name):
            return sqw[:, W_NAMES.index(name), :]

        s_ctx = sem("ctx_loaded")
        s_x = [sem(f"x_loaded{b}") for b in range(B)]
        s_sq = sem("square_weights_loaded")
        s_cst = sem("constants_loaded")
        s_cstb = sem("bias_factors_loaded")
        s_h = sem("first_norm")
        s_rows = sem("row_loads")
        s_blank = [sem(f"blank_rows{m}") for m in range(2)]
        s_w2 = [sem(f"second_weights{m}") for m in range(2)]
        s_w1 = [sem(f"first_weights_piece{k}") for k in range(PIECES)]
        s_w1hi = [sem(f"first_weights_high{m}") for m in range(2)]
        s_w1lo = [sem(f"first_weights_low{m}") for m in range(2)]
        s_xhi = [sem(f"expert_rows_high{m}") for m in range(2)]
        s_set = sem("constants_set")
        s_iset = sem("ident_steps")
        s_dve = sem("dve_order")
        s_pool = sem("pool_order")
        s_var = sem("variances")
        s_rstd = sem("rstd_ready")
        s_ctxn = sem("ctx_normed")
        s_ctxT = sem("ctx_transposed")
        s_kin = sem("kv_input")
        s_kv = sem("kv_projected")
        s_kvsb = sem("kv_in_sbuf")
        s_kvfree = sem("kv_banks_read")
        s_norm = sem("tokens_normed")
        s_inTp = sem("tokens_transposed")
        s_inT = sem("tokens_T_in_sbuf")
        s_q = sem("q_projected")
        s_rope = sem("rope_parts")
        s_qsum = sem("q_rotated")
        s_qhi = sem("q_high")
        s_qlo = sem("q_low")
        s_qrep = sem("q_stacked")
        s_qstA = sem("q_stack_half_ACT")
        s_qstD = sem("q_stack_half_DVE")
        s_ksplit = sem("k_parts")
        s_kones = sem("k_stack_last_rows")
        s_krep = sem("k_stacked")
        s_krepsb = sem("k_stacked_in_sbuf")
        s_sc = [sem(f"scores{m}") for m in range(2)]
        s_peak = [sem(f"maxima{m}") for m in range(2)]
        s_pkT = [sem(f"maxima_transposed{m}") for m in range(2)]
        s_pkTsb = [sem(f"maxima_in_stack{m}") for m in range(2)]
        s_st = [sem(f"shifted_scores{m}") for m in range(2)]
        s_exp = [sem(f"probs{m}") for m in range(2)]
        s_bhigh = sem("bias_factors_high")
        s_bfac = sem("bias_factors")
        s_pv = [sem(f"attended{m}") for m in range(2)]
        s_nd = [sem(f"attended_in_sbuf{m}") for m in range(2)]
        s_att = [sem(f"attT_ready{m}") for m in range(2)]
        s_yT = sem("yT_in_sbuf")
        s_yz = sem("y_projected")
        s_yread = sem("y_read")
        s_z = sem("gate_projected")
        s_tanh = sem("gate_tanh")
        s_hbase = sem("residual_ready")
        s_hidk = [sem(f"moe_rows{m}") for m in range(2)]
        s_base = sem("base_ready")
        s_pair = [sem(f"pair_numbers{m}") for m in range(2)]
        s_hid = [sem(f"moe_input{m}") for m in range(2)]
        s_hTp = [sem(f"moe_input_T{m}") for m in range(2)]
        s_hTsb = [sem(f"moe_input_T_sbuf{m}") for m in range(2)]
        s_log = [sem(f"logits{m}") for m in range(2)]
        s_dif = [sem(f"weight_difference{m}") for m in range(2)]
        s_wexp = [sem(f"weight_exp{m}") for m in range(2)]
        s_pick = [sem(f"picked{m}") for m in range(2)]
        s_rank = [sem(f"ranks{m}") for m in range(2)]
        s_slot = [sem(f"slots{m}") for m in range(2)]
        s_sent = [sem(f"rows_sent{m}") for m in range(2)]
        s_xe = [sem(f"expert_rows{e}") for e in range(E)]
        s_xT = [sem(f"expert_rows_T{m}") for m in range(2)]
        s_xTsb = [sem(f"expert_rows_T_sbuf{m}") for m in range(2)]
        s_up = [sem(f"expert_up{m}") for m in range(2)]
        s_silu = [sem(f"expert_silu{m}") for m in range(2)]
        s_down = [sem(f"expert_down{m}") for m in range(2)]
        s_ye = [sem(f"expert_out{m}") for m in range(2)]
        s_back = [sem(f"rows_back{m}") for m in range(2)]
        s_got = [sem(f"rows_gathered{t}") for t in range(TILES)]
        s_sum = [sem(f"block_sum{m}") for m in range(2)]
        s_most = sem("fullest_expert")
        s_oorder = sem("overflow_order")
        s_oup = sem("overflow_up")
        s_osilu = sem("overflow_silu")
        s_odown = sem("overflow_down")
        s_osum = sem("overflow_summed")
        s_out = sem("output_written")

        CAP = [SLOT, CAP_D]
        EVEN = [c + c % 2 for c in CAP]

        def place(u):
            g, j = divmod(u, UG)
            return g // (GROUPS // B), GQ * g, j

        def stacked(g, i):
            return (qst[0:ST, 2 * i:2 * i + 2, GQ * g:GQ * g + GQ],
                    ps[0:ST, STACK_BANKS[g] + i, :].rearrange("p (j t) -> p j t", j=2))

        def chunk_rows(cap, c):
            return min(P, cap - P * c)

        def overflows(eng):
            eng.wait_ge(s_most, 1)
            return eng.If(eng.value_load(mostu[0:1, 0:1], min_val=0, max_val=B * T) > SLOT)

        block = stack.enter_context(nc.Block())

        @block.sync
        def _(sp):
            xt = x.rearrange("b (t p) d -> p (b t) d", p=P)
            sp.dma_start(ctxs[:], ctx.rearrange("b k d -> k b d")).then_inc(s_ctx, 16)
            for b in range(B):
                sp.dma_start(xres[:, TB * b:TB * b + TB, :], xt[:, TB * b:TB * b + TB, :]).then_inc(s_x[b], 16)
            square = sq.rearrange("p (n d) -> p n d", d=D)
            sp.dma_start(sqw[:, 0:W_FIRST, :], square[:, 0:W_FIRST, :]).then_inc(s_sq, 16)
            sp.dma_start(sqw[:, W_FIRST:, :], square[:, W_FIRST:, :]).then_inc(s_rows, 16)
            sp.dma_start(row[:], rows.broadcast_to([P, R_END])).then_inc(s_rows, 16)
            sp.dma_start(router[:, 0, :], wg).then_inc(s_rows, 16)
            sp.dma_start(router[:, 1, :], wr).then_inc(s_rows, 16)

            def blanks(m):
                for e in range(E):
                    sp.dma_start(sent[m][e * SLOT:(e + 1) * SLOT, :].rearrange("(c p) d -> p c d", p=P),
                                 blank[:]).then_inc(s_blank[m], 16)
                for n in range(TILES):
                    sp.dma_start(back[m][n * GQ:(n + 1) * GQ, :].rearrange("(c p) d -> p c d", p=P),
                                 blank[:, 0:K2, 0:D]).then_inc(s_blank[m], 16)

            def first_weights(m, k):
                if k >= RAWS:
                    sp.wait_ge(s_w1lo[m], k - RAWS + 1)
                w = (w1b, w1d)[m].rearrange("p (n e f) -> p n e f", e=PIECE, f=FF)
                sp.dma_start(raw[:, k % RAWS], w[:, k]).then_inc(s_w1[k], 16)

            sp.wait_ge(s_set, 2)
            blanks(0)
            for k in range(RAWS):
                first_weights(0, k)
            sp.dma_start(w2[:], w2b.rearrange("p (e c d) -> p e c d", e=E, c=FC)).then_inc(s_w2[0], 16)
            blanks(1)
            for k in range(RAWS, PIECES):
                first_weights(0, k)
            for m in range(2):
                sp.wait_ge(s_sent[m], 16 * NPAIR // P)
                for e in range(E):
                    if m == 1:
                        sp.wait_ge(s_pair[0], e + 1)
                        sp.wait_ge(s_xT[0], e + 1)
                    sp.dma_start(xe[:, e, :, :], sent[m][e * SLOT:(e + 1) * SLOT, :]
                                 .rearrange("(c p) d -> p c d", p=P)).then_inc(s_xe[e], 16)
                sp.wait_ge(s_back[m], 16 * E * SC)
                for g in range(GROUPS):
                    if m == 1:
                        sp.wait_ge(s_sum[0], GT * (g + 1))
                    sp.dma_start(got[:, GT * g:GT * g + GT, :, :],
                                 back[m][g * GQ * K2:(g + 1) * GQ * K2, :].rearrange("(t p k) d -> p t k d", p=P, k=K2))\
                      .then_inc(s_got[g], 16)
                if m == 0:
                    sp.wait_ge(s_down[0], E)
                    sp.wait_ge(s_sum[0], 1)
                    for k in range(RAWS):
                        first_weights(1, k)
                    sp.dma_start(w2[:], w2d.rearrange("p (e c d) -> p e c d", e=E, c=FC)).then_inc(s_w2[1], 16)
                    for k in range(RAWS, PIECES):
                        first_weights(1, k)
            ot = out.rearrange("b (t p) d -> p (b t) d", p=P)
            for g in range(GROUPS):
                sp.wait_ge(s_sum[1], GT * (g + 1))
                sp.dma_start(ot[:, GT * g:GT * g + GT, :], xres[:, GT * g:GT * g + GT, :]).then_inc(s_out, 16)
            sp.wait_ge(s_out, 16 * GROUPS)

        @block.gpsimd
        def _(pool):
            pool.memset(power[:], -0.5).then_inc(s_iset, 1)
            pool.memset(ident[:], 0.0).then_inc(s_iset, 1)
            pool.memset(tri[:], 1.0).then_inc(s_iset, 1)
            pool.memset(ones[:], 1.0).then_inc(s_iset, 1)
            pool.memset(onepad[:], 0.0).then_inc(s_iset, 1)
            pool.memset(vpad[:], 0.0).then_inc(s_iset, 1)
            pool.memset(one[:], 1.0).then_inc(s_iset, 1)
            pool.memset(sel[:].bitcast(F32), 0.0).then_inc(s_iset, 1)
            pool.memset(blank[:, :, 0:D], 0.0).then_inc(s_set, 1)
            pool.memset(blank[:, :, D:ROW], float(NPAIR)).then_inc(s_set, 1)
            pool.wait_ge(s_iset, 8)
            pool.affine_select(out=ident[:], in_=ident[:], compare_op=ALU.not_equal, fill=1.0, base=0,
                               pattern=[[-1, P]], channel_multiplier=1).then_inc(s_set, 1)

            step = [0]

            def link(ins):
                step[0] += 1
                ins.then_inc(s_pool, 1)
                pool.wait_ge(s_pool, step[0])

            count = [0]

            def deviations(var, parts=P):
                count[0] += 1
                pool.wait_ge(s_var, count[0])
                link(pool.tensor_scalar_add(vare[0:parts, var], mv[0:parts, var, 1], EPS))
                pool.tensor_tensor(rstd[0:parts, var], vare[0:parts, var], power[0:parts, var],
                                   ALU.pow).then_inc(s_rstd, 1)

            def of_batch(b):
                return slice(TB * b, TB * b + TB)

            def of_group(g):
                return slice(GT * g, GT * g + GT)

            def send(m, g):
                pool.wait_ge(s_slot[m], g + 1)
                pool.wait_ge(s_hidk[m], g + 1)
                if g == 0:
                    pool.wait_ge(s_blank[m], 16 * (E + TILES))
                for t in range(GT * g, GT * g + GT):
                    for k in range(K2):
                        pool.indirect_dma_start(
                            sent[m], bass.IndirectOffsetOnAxis(ap=slotu[:, t, k:k + 1], axis=0),
                            hidk[:, t, k, :], None, bounds_check=NSLOT - 1, oob_is_err=False).then_inc(s_sent[m], 16)

            def residual(g):
                pool.wait_ge(s_hid[1], g + 1)
                pool.tensor_tensor(base[:, of_group(g), :], xres[:, of_group(g), :], hidk[:, of_group(g), 0, 0:D],
                                   ALU.add).then_inc(s_base, 1)

            def low_weights(m, k):
                pool.wait_ge(s_w1hi[m], k + 1)
                w = slice(PIECE * k, PIECE * k + PIECE)
                pool.tensor_tensor(w1lo[:, w, :], raw[:, k % RAWS], w1hi[:, w, :].bitcast(F32), ALU.subtract)\
                    .then_inc(s_w1lo[m], 1)

            def route(m):
                for u in range(UNITS + max(POOL_STEPS[m].values())):
                    if u in WEIGHT_TURNS[m]:
                        low_weights(m, WEIGHT_TURNS[m].index(u))
                    for name, g in due(POOL_STEPS[m], u):
                        if name == "deviation":
                            deviations(of_group(g))
                        elif name == "residual":
                            if m == 1:
                                residual(g)
                        else:
                            send(m, g)

            def give_back(m):
                for e in range(E):
                    pool.wait_ge(s_xe[e], 16 * (m + 1))
                    if m == 1:
                        pool.wait_ge(s_back[0], 16 * E * SC)
                    pool.tensor_copy(pairu[:, e, :], xe[:, e, :, D]).then_inc(s_pair[m], 1)
                for e in range(E):
                    pool.wait_ge(s_pair[m], e + 1)
                    pool.wait_ge(s_ye[m], e + 1)
                    for c in range(SC):
                        n = chunk_rows(CAP[m], c)
                        pool.indirect_dma_start(
                            back[m], bass.IndirectOffsetOnAxis(ap=pairu[0:n, e, c:c + 1], axis=0),
                            ye[0:n, e, c, :], None, bounds_check=NPAIR - 1, oob_is_err=False).then_inc(s_back[m], 16)

            def rotary_sum(g):
                pool.wait_ge(s_rope, g + 1)
                q = q32[:, g % 2, :]
                pool.tensor_tensor(q, q, ropeb[:, g % 2, :], ALU.add).then_inc(s_qsum, 1)

            def low_queries(g):
                pool.wait_ge(s_qhi, g + 1)
                if g >= 2:
                    pool.wait_ge(s_qrep, g - 1)
                pool.tensor_tensor(qlo[:, g % 2, :], q32[:, g % 2, :], qhi[:, g % 2, :].bitcast(F32), ALU.subtract)\
                    .then_inc(s_qlo, 1)

            deviations(slice(0, B), KV)
            for b in range(B):
                deviations(of_batch(b))
            pool.affine_select(out=tri[:], in_=tri[:], compare_op=ALU.is_gt, fill=0.0, base=0,
                               pattern=[[1, P]], channel_multiplier=-1).then_inc(s_set, 1)
            for j in range(4):
                pool.memset(onepad[:, j, DH * j:DH * j + DH], 1.0).then_inc(s_set, 1)
            pool.wait_ge(s_set, 3)
            blocks = ident[:].rearrange("p (j c) -> p j c", j=UG)
            n = ST // 3
            pool.tensor_copy(sel[:, 0, :, 0:n], blocks).then_inc(s_set, 1)
            pool.tensor_copy(sel[:, 1, :, n:2 * n], blocks).then_inc(s_set, 1)
            pool.tensor_copy(sel[:, 0, :, 2 * n:3 * n], blocks).then_inc(s_set, 1)
            for b in range(B):
                deviations(of_batch(b))
            for g in range(GROUPS):
                rotary_sum(g)
                low_queries(g)
            pool.wait_ge(s_rows, 64)
            pool.wait_ge(s_cst, 32)
            for b in range(B):
                s = of_batch(b)
                pool.tensor_tensor(base[:, s, :], xres[:, s, :], hid[:, s, :], ALU.add).then_inc(s_hbase, 1)
                pool.tensor_tensor(hidb[:, s, :], hid[:, s, :],
                                   row[:, R_BOUT:R_BOUT + D].unsqueeze(1).broadcast_to([P, TB, D]),
                                   ALU.subtract).then_inc(s_hbase, 1)
            pool.tensor_copy(hidk[:, :, :, D], cst[:, C_PAIR:C_PAIR + TILES * K2].rearrange("p (t k) -> p t k", k=K2))\
                .then_inc(s_pool, 1)
            step[0] += 1
            pool.wait_ge(s_pool, step[0])
            route(0)
            give_back(0)
            for g in range(GROUPS):
                deviations(of_group(g))
            route(1)
            give_back(1)

        @block.scalar
        def _(act):
            act.dma_start(col[:], cols).then_inc(s_cst, 16)
            act.dma_start(cst[:, 0:C_BROW], consts[:, 0:C_BROW]).then_inc(s_cst, 16)
            act.dma_start(cst[:, C_BROW:C_END], consts[:, C_BROW:C_END]).then_inc(s_cstb, 16)
            act.wait_ge(s_cst, 32)
            for b in range(B):
                own = cst[ST:ST + Q4, C_MASK:C_MASK + Q4].unsqueeze(1).unsqueeze(3).broadcast_to([Q4, UG, Q4, KP])
                act.activation(kst[ST:ST + Q4, b].rearrange("p (j q) k -> p j q k", j=UG), own, ACT.Identity)\
                   .then_inc(s_kones, 1)

            def high_weights(m, k):
                act.wait_ge(s_w1[k], 16 * (m + 1))
                act.copy(w1hi[:, PIECE * k:PIECE * k + PIECE, :], raw[:, k % RAWS]).then_inc(s_w1hi[m], 1)

            def load_table(func, n):
                act.activation(spare[0:1, n:n + 1], one[0:1, 0:1], func)

            def maxima(a, u):
                b, at, j = place(u)
                act.wait_ge(s_pkT[a], u + 1)
                act.copy(qst[ST:ST + Q4, j, at:at + GQ], ps[ST:ST + Q4, BK + u % 2, 0:GQ]).then_inc(s_pkTsb[a], 1)

            def attention(a, u):
                if u == 0:
                    maxima(a, 0)
                g, rest = divmod(u - AHEAD - 1, UG)
                if rest == UG - 1 and 0 <= g < GROUPS:
                    act.wait_ge(s_pv[a], UG * (g + 1))
                    if g >= 1:
                        act.wait_ge(s_att[a], g)
                    act.copy(numden, ps[:, BNUM:BDEN + 1, 0:GQ]).then_inc(s_nd[a], 1)
                if u < UNITS:
                    act.wait_ge(s_st[a], u + 1)
                    if u >= RING:
                        act.wait_ge(s_pv[a], u - RING + 1)
                    act.activation(probT[0:KV, u % RING].rearrange("p (i q) t -> p i (q t)", i=2),
                                   ps[0:KV, BK:BK + 2, :], ACT.Exp).then_inc(s_exp[a], 1)
                if u + 1 < UNITS:
                    maxima(a, u + 1)

            def tanh(a, g):
                act.wait_ge(s_z, g + 1)
                act.activation(norm[:, GT * g:GT * g + GT, :], ps[:, BY, 0:GQ].rearrange("p (t d) -> p t d", t=GT),
                               ACT.Tanh, scale=0.5).then_inc(s_tanh, 1)

            def projected(a, g):
                act.wait_ge(s_yz, g + 1)
                act.activation(yT, ps[:, BY, 0:GQ], ACT.Identity, bias=col[:, V_BOUT:V_BOUT + 1]).then_inc(s_yT, 1)

            def copies(m, g):
                act.wait_ge(s_hid[m], g + 1)
                s = slice(GT * g, GT * g + GT)
                act.copy(hidk[:, s, 1, 0:D], hidk[:, s, 0, 0:D]).then_inc(s_hidk[m], 1)

            def turned(m, g):
                act.wait_ge(s_hTp[m], g + 1)
                b, at = divmod(g, GROUPS // B)
                act.copy(inT[:, b, GQ * at:GQ * at + GQ], ps[:, BR, 0:GQ]).then_inc(s_hTsb[m], 1)

            def weights(m):
                act.wait_ge(s_dif[m], GROUPS)
                act.activation(wexp[:], wdif[:], ACT.Exp).then_inc(s_wexp[m], 1)

            steps = dict(projected=projected, tanh=tanh, copies=copies, turned=turned)

            def experts(m):
                act.wait_ge(s_w1lo[m], PIECES)
                for e in range(E):
                    for f in range(FC):
                        n = FC * e + f
                        act.wait_ge(s_up[m], n + 1)
                        if e >= 2:
                            act.wait_ge(s_down[m], e - 1)
                        bias = col[:, V_B1 + n:V_B1 + n + 1] if m == 0 else 0.0
                        act.activation(hT[:, e % 2, f, 0:CAP[m]], ps[:, 2 + n % 4, 0:CAP[m]], ACT.Silu,
                                       bias=bias).then_inc(s_silu[m], 1)

            def keys_out(a):
                act.wait_ge(s_krep, a + 1)
                rep = ps[0:ST, BNUM:BNUM + 2, :].rearrange("p i (j c) -> p (i j) c", j=2)
                act.copy(krep[:], rep[:, :, 0:B * KP]).then_inc(s_krepsb, 1)

            def attention_input(a, g):
                act.wait_ge(s_inTp, GROUPS * a + g + 1)
                b, at = divmod(g, GROUPS // B)
                dst = inT[:, b, GQ * at:GQ * at + GQ]
                if a == 0:
                    act.activation(dst, ps[:, tokens_bank(g), 0:GQ], ACT.Identity, scale=col[:, V_GAMMA:V_GAMMA + 1],
                                   bias=col[:, V_BETA:V_BETA + 1]).then_inc(s_inT, 1)
                else:
                    act.copy(dst, ps[:, tokens_bank(g), 0:GQ]).then_inc(s_inT, 1)

            def high_queries(a, g):
                if g >= 2:
                    act.wait_ge(s_qrep, GROUPS * a + g - 1)
                if a == 0:
                    act.wait_ge(s_qsum, g + 1)
                    act.copy(qhi[:, g % 2, :], q32[:, g % 2, :]).then_inc(s_qhi, 1)
                else:
                    act.wait_ge(s_q, GROUPS + g + 1)
                    act.activation(qhi[:, g % 2, :], ps[:, queries_bank(g), 0:GQ], ACT.Identity,
                                   bias=col[:, V_BQ:V_BQ + 1]).then_inc(s_qhi, 1)

            def stack_half(a, g):
                act.wait_ge(s_qrep, GROUPS * a + g + 1)
                act.copy(*stacked(g, 0)).then_inc(s_qstA, 1)

            def query_steps(a, turn):
                for name, g in at_turn(ACT_QUERIES[a], turn):
                    if name == "tokens":
                        attention_input(a, g)
                    elif name == "high":
                        high_queries(a, g)
                    elif name == "stack":
                        stack_half(a, g)
                    elif a == 0:
                        keys_out(0)

            for a in range(2):
                query_steps(a, -1)
                load_table(ACT.Exp, 2 + a)
                for u in range(UNITS + max(ACT_STEPS[a].values())):
                    query_steps(a, u)
                    attention(a, u)
                    if u in WEIGHT_TURNS[a]:
                        high_weights(a, WEIGHT_TURNS[a].index(u))
                    for name, g in due(ACT_STEPS[a], u):
                        steps[name](a, g)
                if a == 0:
                    keys_out(1)
                weights(a)
                load_table(ACT.Silu, a)
                experts(a)
                if a == 0:
                    with overflows(act):
                        for e in range(E):
                            for b in range(B):
                                n = B * e + b
                                for f in range(FC):
                                    act.wait_ge(s_oup, FC * n + f + 1)
                                    if f == 0 and n >= 1:
                                        act.wait_ge(s_odown, n)
                                    act.activation(overh[:, f, :], ps[:, f, :], ACT.Silu,
                                                   bias=col[:, V_B1 + FC * e + f:V_B1 + FC * e + f + 1])\
                                       .then_inc(s_osilu, 1)

        @block.vector
        def _(dve):
            order = {s_dve: 0, s_oorder: 0}

            def link(ins, on=s_dve):
                order[on] += 1
                ins.then_inc(on, 1)
                dve.wait_ge(on, order[on])

            def variances(src, n, at, parts=P):
                for k in range(n):
                    last = dve.bn_stats(stats[0:parts, at + k, :], src[:, k, :])
                link(last)
                for k in range(n):
                    last = dve.bn_aggr(mv[0:parts, at + k, :], stats[0:parts, at + k, :])
                last.then_inc(s_var, 1)

            group = [0]

            def normed(dst, src, n, at, parts=P):
                group[0] += 1
                dve.wait_ge(s_rstd, group[0])
                for k in range(n):
                    last = dve.tensor_scalar(dst[:, k, :], src[:, k, :], mv[0:parts, at + k, 0:1],
                                             rstd[0:parts, at + k:at + k + 1], ALU.subtract, ALU.mult)
                return last

            def attention(a, u):
                if u < UNITS:
                    dve.wait_ge(s_sc[a], u + 1)
                    s = ps[:, BS:BS + 2, 0:Q4 * KP].rearrange("p i (q k) -> p i q k", q=Q4)[:, :, :, 0:KV]
                    dve.tensor_reduce(peak[:, u % 2], s, AX.X, ALU.max, negate=True).then_inc(s_peak[a], 1)

            def rows_of(g):
                return slice(GT * g, GT * g + GT)

            def attended(a, g):
                dve.wait_ge(s_nd[a], g + 1)
                b, at = divmod(g, GROUPS // B)
                link(dve.reciprocal(rden, numden[:, 1]))
                dve.tensor_tensor(attT[:, b, GQ * at:GQ * at + GQ], numden[:, 0], rden, ALU.mult)\
                   .then_inc(s_att[a], 1)

            def projected(a, g):
                dve.wait_ge(s_yz, g + 1)
                dve.wait_ge(s_yT, g + 1)
                if g == 0:
                    dve.wait_ge(s_hbase, 2 * B)
                dve.tensor_tensor(ytok[:, rows_of(g), :], ps[:, BY, GQ:2 * GQ].rearrange("p (t d) -> p t d", t=GT),
                                  hidb[:, rows_of(g), :], ALU.subtract).then_inc(s_yread, 1)

            def residual(a, g):
                s = rows_of(g)
                if a == 0:
                    dve.wait_ge(s_tanh, g + 1)
                    dve.wait_ge(s_yread, g + 1)
                    link(dve.scalar_tensor_tensor(out=ytok[:, s, :], in0=norm[:, s, :], scalar=1.0, in1=ytok[:, s, :],
                                                  op0=ALU.add, op1=ALU.mult))
                    link(dve.scalar_tensor_tensor(out=xres[:, s, :], in0=ytok[:, s, :], scalar=0.5, in1=base[:, s, :],
                                                  op0=ALU.mult, op1=ALU.add))
                else:
                    dve.wait_ge(s_yz, GROUPS + g + 1)
                    bo = row[:, R_BO:R_BO + D].unsqueeze(1).broadcast_to([P, GT, D])
                    dve.tensor_tensor(ytok[:, s, :], ps[:, BY, 0:GQ].rearrange("p (t d) -> p t d", t=GT), bo, ALU.add)\
                       .then_inc(s_yread, 1)
                    dve.wait_ge(s_yread, GROUPS + g + 1)
                    link(dve.tensor_tensor(xres[:, s, :], xres[:, s, :], ytok[:, s, :], ALU.add))
                variances(xres[:, s, :], GT, GT * g)

            def hidden(m, g):
                if m == 1 and g == 0:
                    dve.wait_ge(s_sent[0], 16 * NPAIR // P)
                normed(hidk[:, rows_of(g), 0, 0:D], xres[:, rows_of(g), :], GT, GT * g).then_inc(s_hid[m], 1)

            def choose(m, g):
                s = rows_of(g)
                dve.wait_ge(s_log[m], g + 1)
                lp = ps[:, BR, 0:GT * E].rearrange("p (t e) -> p t e", t=GT)
                if m == 0:
                    bg = gbias[:].unsqueeze(1).broadcast_to([P, GT, E])
                    link(dve.scalar_tensor_tensor(out=logit[:, s, :], in0=lp, scalar=GATE_DIV, in1=bg,
                                                  op0=ALU.mult, op1=ALU.add))
                else:
                    link(dve.tensor_copy(logit[:, s, :], lp))
                for t in range(GT * g, GT * g + GT):
                    last = dve.max(top[:, t, :], logit[:, t, :])
                link(last)
                for t in range(GT * g, GT * g + GT):
                    last = dve.max_index(topi[:, t, :], top[:, t, :], logit[:, t, :])
                order[s_dve] += 1
                last.then_inc(s_dve, 1)
                dve.tensor_tensor(wdif[:, s], top[:, s, 1], top[:, s, 0], ALU.subtract).then_inc(s_dif[m], 1)
                dve.wait_ge(s_dve, order[s_dve])
                link(dve.tensor_copy(topf[:, s, :], topi[:, s, 0:K2]))
                iota = cst[:, C_IOTA:C_IOTA + E].unsqueeze(1).unsqueeze(1).broadcast_to([P, GT, K2, E])
                link(dve.tensor_tensor(pick[:, s], topf[:, s, :].unsqueeze(3).broadcast_to([P, GT, K2, E]), iota,
                                       ALU.is_equal))
                dve.tensor_tensor(picked[:, s, :], pick[:, s, 0, :], pick[:, s, 1, :], ALU.add).then_inc(s_pick[m], 1)

            def slots(m, g):
                s = rows_of(g)
                dve.wait_ge(s_rank[m], g + 1)
                rp = ps[:, BR, P:P + GT * E].rearrange("p (t e) -> p t e", t=GT)
                link(dve.tensor_tensor(ranked[:, s], pick[:, s], rp.unsqueeze(2).broadcast_to([P, GT, K2, E]), ALU.mult))
                link(dve.tensor_reduce(rank[:, s, :], ranked[:, s], AX.X, ALU.add))
                dve.tensor_scalar(over[:, s, :], rank[:, s, :], float(CAP[m]), float(NSLOT), ALU.is_ge, ALU.mult)
                link(dve.scalar_tensor_tensor(out=slot[:, s, :], in0=topf[:, s, :], scalar=float(SLOT),
                                              in1=rank[:, s, :], op0=ALU.mult, op1=ALU.add))
                dve.tensor_tensor(slotu[:, s, :], slot[:, s, :], over[:, s, :], ALU.add).then_inc(s_slot[m], 1)
                if m == 0 and g == GROUPS - 1:
                    link(dve.tensor_reduce(most[:], ps[:, BR, 2 * P:2 * P + E], AX.X, ALU.max))
                    dve.tensor_copy(mostu[:], most[:]).then_inc(s_most, 1)


            def keys_and_values(a):
                dve.wait_ge(s_kv, a + 1)
                kp = ps[:, 2, 0:B * KV].rearrange("p (b k) -> p b k", b=B)
                k = kT[:, :, 0:KV]
                if a == 0:
                    kr = ps[:, 2, 256:256 + B * KV].rearrange("p (b k) -> p b k", b=B)
                    cos = cst[:, C_COS:C_COS + KV].unsqueeze(1).broadcast_to([P, B, KV])
                    sin = cst[:, C_SIN:C_SIN + KV].unsqueeze(1).broadcast_to([P, B, KV])
                    link(dve.memset(kT[:, :, KV:KP], 0.0))
                    link(dve.scalar_tensor_tensor(out=k, in0=kp, scalar=SCALE, in1=cos, op0=ALU.mult, op1=ALU.mult))
                    link(dve.scalar_tensor_tensor(out=ropek[:], in0=kr, scalar=SCALE, in1=sin, op0=ALU.mult, op1=ALU.mult))
                    link(dve.tensor_tensor(k, k, ropek[:], ALU.add))
                else:
                    link(dve.tensor_scalar(k, kp, col[:, V_BK:V_BK + 1], SCALE, ALU.add, ALU.mult))
                link(dve.tensor_copy(khi[:], kT[:]))
                dve.tensor_tensor(klo[:], kT[:], khi[:].bitcast(F32), ALU.subtract).then_inc(s_ksplit, 1)
                if a == 0:
                    dve.wait_ge(s_iset, 6)
                for b in range(B):
                    v = ps[0:KV, 3, b * D:(b + 1) * D].rearrange("p (g j d) -> p g j d", g=4, j=4)
                    for j in range(4):
                        dst = vpad[:, b, j:H:4, DH * j:DH * j + DH]
                        if a == 0:
                            last = dve.tensor_copy(dst, v[:, :, j, :])
                        else:
                            bv = row[0:KV, R_BV:R_BV + D].rearrange("p (g j d) -> p g j d", g=4, j=4)
                            last = dve.tensor_tensor(dst, v[:, :, j, :], bv[:, :, j, :], ALU.add)
                last.then_inc(s_kvfree, 1)

            def stack_keys(a, b):
                dve.wait_ge(s_krepsb, a + 1)
                own = cst[0:ST, C_MASK:C_MASK + Q4].unsqueeze(1).unsqueeze(3).broadcast_to([ST, UG, Q4, KP])
                dve.tensor_tensor(kst[0:ST, b].rearrange("p (j q) k -> p j q k", j=UG),
                                  krep[:, :, b * KP:(b + 1) * KP].unsqueeze(2).broadcast_to([ST, UG, Q4, KP]), own,
                                  ALU.mult).then_inc(s_kvsb, 1)

            def next_context(m, g):
                if g == GROUPS - 1:
                    dve.wait_ge(s_ctxT, 2)
                    dve.tensor_copy(kinT[:], ps[:, BS, 0:B * KV].rearrange("p (b k) -> p b k", b=B)).then_inc(s_kin, 1)

            def next_parts(m, g):
                if g == GROUPS - 1:
                    keys_and_values(1)

            def next_keys(m, g):
                if g == GROUPS - 1:
                    for b in range(B):
                        stack_keys(1, b)

            steps = dict(attended=attended, projected=projected, residual=residual, hidden=hidden,
                         choose=choose, slots=slots, next_context=next_context, next_parts=next_parts,
                         next_keys=next_keys)

            def queries(g):
                at = GQ * (g % (GROUPS // B))
                dve.wait_ge(s_q, g + 1)
                if g >= 2:
                    dve.wait_ge(s_qlo, g - 1)
                dve.tensor_tensor(q32[:, g % 2, :], ps[:, queries_bank(g), 0:GQ], cst[:, C_COS + at:C_COS + at + GQ], ALU.mult)
                dve.tensor_tensor(ropeb[:, g % 2, :], ps[:, queries_bank(g), GQ:2 * GQ], cst[:, C_SIN + at:C_SIN + at + GQ],
                                  ALU.mult).then_inc(s_rope, 1)

            def low_queries(g):
                dve.wait_ge(s_qhi, GROUPS + g + 1)
                if g >= 2:
                    dve.wait_ge(s_qrep, GROUPS + g - 1)
                dve.scalar_tensor_tensor(out=qlo[:, g % 2, :], in0=ps[:, queries_bank(g), 0:GQ], scalar=col[:, V_BQ:V_BQ + 1],
                                         in1=qhi[:, g % 2, :].bitcast(F32), op0=ALU.add, op1=ALU.subtract)\
                   .then_inc(s_qlo, 1)

            def stack_half(a, g):
                dve.wait_ge(s_qrep, GROUPS * a + g + 1)
                dve.tensor_copy(*stacked(g, 1)).then_inc(s_qstD, 1)

            def experts(m):
                def rows(e):
                    dve.wait_ge(s_xT[m], e + 1)
                    if e >= 2:
                        dve.wait_ge(s_up[m], FC * (e - 1))
                    x = ps[:, e % 2, 0:EVEN[m]]
                    dve.tensor_copy(xhi[:, e % 2, 0:EVEN[m]], x).then_inc(s_xhi[m], 1)
                    dve.wait_ge(s_xhi[m], e + 1)
                    dve.tensor_tensor(xlo[:, e % 2, 0:EVEN[m]], x, xhi[:, e % 2, 0:EVEN[m]].bitcast(F32), ALU.subtract)\
                       .then_inc(s_xTsb[m], 1)

                def outputs(e):
                    dve.wait_ge(s_down[m], e + 1)
                    if m == 1 and e == 0:
                        dve.wait_ge(s_back[0], 16 * E * SC)
                    for c in range(SC):
                        n = chunk_rows(CAP[m], c)
                        src = ps[0:n, 6 + e % 2, c * P:(c + 1) * P]
                        if m == 0:
                            last = dve.tensor_tensor(ye[0:n, e, c, :], src, row[0:n, R_B2 + e * D:R_B2 + (e + 1) * D],
                                                     ALU.add)
                        else:
                            last = dve.tensor_copy(ye[0:n, e, c, :], src)
                    last.then_inc(s_ye[m], 1)

                def weights():
                    dve.wait_ge(s_wexp[m], 1)
                    link(dve.tensor_scalar(wden[:], wexp[:], 1.0, None, ALU.add))
                    link(dve.reciprocal(wtok[:, :, 0], wden[:]))
                    link(dve.tensor_tensor(wtok[:, :, 1], wexp[:], wtok[:, :, 0], ALU.mult))

                weights()
                rows(0)
                for e in range(E + 1):
                    if e + 1 < E:
                        rows(e + 1)
                    if e >= 1:
                        outputs(e - 1)

            def combine(m, g):
                src = xres if m == 0 else base
                dve.wait_ge(s_got[g], 16 * (m + 1))
                if m == 1:
                    dve.wait_ge(s_base, g + 1)
                tiles = range(GT * g, GT * g + GT)
                for t in tiles:
                    last = dve.scalar_tensor_tensor(out=norm[:, t, :], in0=got[:, t, 0, :], scalar=wtok[:, t, 0:1],
                                                    in1=src[:, t, :], op0=ALU.mult, op1=ALU.add)
                link(last)
                for t in tiles:
                    dve.scalar_tensor_tensor(out=xres[:, t, :], in0=got[:, t, 1, :], scalar=wtok[:, t, 1:2],
                                             in1=norm[:, t, :], op0=ALU.mult, op1=ALU.add).then_inc(s_sum[m], 1)

            def before_attention(g):
                combine(0, g)
                dve.wait_ge(s_sum[0], GT * (g + 1))
                variances(xres[:, rows_of(g), :], GT, GT * g)

            def attention_norm(g):
                normed(norm[:, rows_of(g), :], xres[:, rows_of(g), :], GT, GT * g).then_inc(s_norm, 1)

            def bias_parts():
                dve.wait_ge(s_cstb, 16)
                by_key = cst[:, C_BROW:C_BROW + TB * KP].rearrange("p (t k) -> p t k", t=TB)
                dve.tensor_copy(btok[:], cst[:, C_BCOL:C_BCOL + TB * P].rearrange("p (t k) -> p t k", t=TB)).then_inc(s_bfac, 1)
                dve.tensor_copy(bkey[:], by_key).then_inc(s_bhigh, 1)
                dve.wait_ge(s_bhigh, 1)
                dve.tensor_tensor(bkey[LOW:P], by_key[LOW:P], bkey[LOW:P].bitcast(F32), ALU.subtract).then_inc(s_bfac, 1)

            dve.wait_ge(s_ctx, 16)
            variances(ctxs[:], B, 0, KV)
            normed(ctxn[:], ctxs[:], B, 0, KV).then_inc(s_ctxn, 1)
            dve.wait_ge(s_ctxn, 1)
            for b in range(B):
                dve.wait_ge(s_x[b], 16)
                variances(xres[:, TB * b:TB * b + TB, :], TB, TB * b)
            for b in range(B):
                s = slice(TB * b, TB * b + TB)
                normed(hid[:, s, :], xres[:, s, :], TB, TB * b).then_inc(s_h, 1)
                dve.wait_ge(s_h, b + 1)
                variances(hid[:, s, :], TB, TB * b)
            dve.wait_ge(s_cst, 32)
            dve.wait_ge(s_ctxT, 1)
            dve.tensor_scalar(kinT[:], ps[:, 0, 0:B * KV].rearrange("p (b k) -> p b k", b=B),
                              col[:, V_GAMMA:V_GAMMA + 1], col[:, V_BETA:V_BETA + 1], ALU.mult, ALU.add)\
               .then_inc(s_kin, 1)
            for b in range(B):
                s = slice(TB * b, TB * b + TB)
                normed(norm[:, s, :], hid[:, s, :], TB, TB * b).then_inc(s_norm, 1)
                if b == 0:
                    keys_and_values(0)
            def query_steps(a, turn):
                for name, g in at_turn(DVE_QUERIES[a], turn):
                    if name == "sum":
                        before_attention(g)
                    elif name == "norm":
                        attention_norm(g)
                    elif name == "rotated":
                        queries(g)
                    elif name == "low":
                        low_queries(g)
                    elif name == "stack":
                        stack_half(a, g)
                    elif name == "keys":
                        stack_keys(0, g)
                    else:
                        bias_parts()

            query_steps(0, -1)
            dve.wait_ge(s_rows, 64)
            link(dve.tensor_scalar(gbias[:], row[:, R_BG:R_BG + E], GATE_DIV, None, ALU.mult))
            for u in range(UNITS + max(DVE_STEPS[0].values())):
                attention(0, u)
                query_steps(0, u)
                for name, g in due(DVE_STEPS[0], u):
                    steps[name](0, g)
            experts(0)
            with overflows(dve):
                link(dve.tensor_tensor(ranked[:], pick[:], over[:].unsqueeze(3).broadcast_to([P, TILES, K2, E]),
                                       ALU.mult), s_oorder)
                link(dve.tensor_tensor(ranked[:], ranked[:], wtok[:].unsqueeze(3).broadcast_to([P, TILES, K2, E]),
                                       ALU.mult), s_oorder)
                link(dve.tensor_tensor(wover[:], ranked[:, :, 0, :], ranked[:, :, 1, :], ALU.add), s_oorder)
                link(dve.tensor_scalar(wover[:], wover[:], 1.0 / NSLOT, None, ALU.mult), s_oorder)
                for e in range(E):
                    b2 = row[:, R_B2 + e * D:R_B2 + (e + 1) * D].unsqueeze(1).broadcast_to([P, TB, D])
                    for b in range(B):
                        dve.wait_ge(s_odown, B * e + b + 1)
                        y = ytok[:, 0:TB, :]
                        dve.tensor_tensor(y, ps[:, 4, :].rearrange("p (t d) -> p t d", t=TB), b2, ALU.add)\
                           .then_inc(s_osum, 1)
                        dve.wait_ge(s_osum, B * e + b + 1)
                        for k in range(TB):
                            t = TB * b + k
                            last = dve.scalar_tensor_tensor(out=xres[:, t, :], in0=y[:, k, :], scalar=wover[:, t, e:e + 1],
                                                            in1=xres[:, t, :], op0=ALU.mult, op1=ALU.add)
                        link(last, s_oorder)
            query_steps(1, -1)
            for u in range(UNITS + max(DVE_STEPS[1].values())):
                attention(1, u)
                query_steps(1, u)
                for name, g in due(DVE_STEPS[1], u):
                    steps[name](1, g)
            experts(1)
            for g in range(GROUPS):
                combine(1, g)

        @block.tensor
        def _(pe):
            def warm_up(n, bank=BR):
                for _ in range(n):
                    pe.matmul(ps[:, bank, 0:GQ], ident[:], blank[:, 0:2, 0:D], start=True, stop=True)

            def transposed(bank, src, n, parts=P):
                for k in range(n):
                    last = pe.matmul(ps[:, bank, k * parts:(k + 1) * parts], src(k), ident[0:parts, 0:parts],
                                     start=True, stop=True, is_transpose=True)
                return last

            def scores(a, u):
                b, at, j = place(u)
                if j == 0:
                    pe.wait_ge(s_qstA, GROUPS * a + u // UG + 1)
                    pe.wait_ge(s_qstD, GROUPS * a + u // UG + 1)
                if u % (UNITS // B) == 0:
                    pe.wait_ge(s_kvsb, B * a + b + 1)
                if u >= 1:
                    pe.wait_ge(s_peak[a], u)
                for i in range(GT):
                    last = pe.matmul(ps[:, BS + i, 0:Q4 * KP], qst[0:ST, j, at + i * P:at + (i + 1) * P],
                                     kst[0:ST, b, Q4 * j:Q4 * j + Q4, :].rearrange("p q k -> p (q k)"),
                                     start=True, stop=True)
                last.then_inc(s_sc[a], 1)

            def maxima(a, u):
                pe.wait_ge(s_peak[a], u + 1)
                for i in range(GT):
                    last = pe.matmul(ps[ST:ST + Q4, BK + u % 2, i * P:(i + 1) * P], peak[:, u % 2, i, :], ident[:],
                                     start=True, stop=True)
                last.then_inc(s_pkT[a], 1)

            def shifted_scores(a, u):
                b, at, j = place(u)
                pe.wait_ge(s_pkTsb[a], u + 1)
                if u == 0:
                    pe.wait_ge(s_qstA, GROUPS * a + 2)
                    pe.wait_ge(s_qstD, GROUPS * a + 2)
                    if a == 0:
                        pe.wait_ge(s_bfac, 2)
                if u >= 1:
                    pe.wait_ge(s_exp[a], u)
                for q in range(Q4):
                    last = pe.matmul(ps[0:KP, BK + q // 2, GQ * (q % 2):GQ * (q % 2) + GQ],
                                     kst[0:ST + Q4, b, Q4 * j + q, :], qst[0:ST + Q4, j, at:at + GQ],
                                     start=True, stop=(a == 1))
                    for i in range(GT if a == 0 else 0):
                        t = (at // P + i) % TB
                        o = GQ * (q % 2) + i * P
                        last = pe.matmul(ps[0:KP, BK + q // 2, o:o + P], bkey[0:LOW + NEAR, t, :],
                                         btok[0:LOW + NEAR, t, :], start=False, stop=(i == GT - 1))
                last.then_inc(s_st[a], 1)

            def attend(a, u):
                b, at, j = place(u)
                pe.wait_ge(s_exp[a], u + 1)
                if u == 0:
                    pe.wait_ge(s_qstA, GROUPS * (a + 1))
                    pe.wait_ge(s_qstD, GROUPS * (a + 1))
                    pe.wait_ge(s_kvfree, a + 1)
                if j == 0 and u >= UG:
                    pe.wait_ge(s_nd[a], u // UG)
                for bank in (BNUM, BDEN):
                    for q in range(Q4):
                        w = vpad[:, b, Q4 * q + j, :] if bank == BNUM else onepad[:, j, :]
                        last = pe.matmul(ps[32 * q:32 * q + 32, bank, 0:GQ], w, probT[0:KV, u % RING, q, :],
                                         start=(j == 0), stop=(j == UG - 1))
                last.then_inc(s_pv[a], 1)

            def project(a, g):
                pe.wait_ge(s_att[a], g + 1)
                if g >= 1:
                    pe.wait_ge(s_tanh if a == 0 else s_yread, g if a == 0 else GROUPS + g)
                b, at = divmod(g, GROUPS // B)
                q0 = GQ * at
                if a == 0:
                    pe.matmul(ps[:, BY, 0:GQ], weight("out0"), attT[:, b, q0:q0 + GQ], start=True, stop=True)
                for k in range(GT):
                    o = (GQ if a == 0 else 0) + k * D
                    last = pe.matmul(ps[:, BY, o:o + D], attT[:, b, q0 + k * P:q0 + (k + 1) * P],
                                     weight("out0" if a == 0 else "o1"), start=True, stop=True)
                last.then_inc(s_yz, 1)

            def gate(a, g):
                pe.wait_ge(s_yT, g + 1)
                pe.wait_ge(s_yread, g + 1)
                for k in range(GT):
                    z = ps[:, BY, k * D:(k + 1) * D]
                    pe.matmul(z, one[:], row[0:1, R_BGATE:R_BGATE + D], start=True, stop=False)
                    last = pe.matmul(z, yT[:, k * P:(k + 1) * P], weight("gate0"), start=False, stop=True)
                last.then_inc(s_z, 1)

            def turn(m, g):
                pe.wait_ge(s_hid[m], g + 1)
                if g >= 1:
                    pe.wait_ge(s_slot[m], g)
                if m == 1 and g == 0:
                    pe.wait_ge(s_inT, 2 * GROUPS)
                transposed(BR, lambda k: hidk[:, GT * g + k, 0, 0:D], GT).then_inc(s_hTp[m], 1)

            def logits(m, g):
                pe.wait_ge(s_hTsb[m], g + 1)
                b, at = divmod(g, GROUPS // B)
                for k in range(GT):
                    q0 = GQ * at + k * P
                    last = pe.matmul(ps[:, BR, k * E:(k + 1) * E], inT[:, b, q0:q0 + P], router[:, m, :],
                                     start=True, stop=True)
                last.then_inc(s_log[m], 1)

            def ranks(m, g):
                pe.wait_ge(s_pick[m], g + 1)
                for k in range(GT):
                    t = GT * g + k
                    for s in range(t + 1):
                        last = pe.matmul(ps[:, BR, P + k * E:P + (k + 1) * E], tri[:] if s == t else ones[:],
                                         picked[:, s, :], start=(s == 0), stop=(s == t))
                if m == 0 and g == GROUPS - 1:
                    for t in range(TILES):
                        last = pe.matmul(ps[:, BR, 2 * P:2 * P + E], ones[:], picked[:, t, :],
                                         start=(t == 0), stop=(t == TILES - 1))
                last.then_inc(s_rank[m], 1)

            def project_kv(a):
                pe.wait_ge(s_kin, a + 1)
                names = (("k0", 0), ("k0p", 256)) if a == 0 else (("k1", 0),)
                for name, at in names:
                    pe.matmul(ps[:, 2, at:at + B * KV], weight(name), kinT[:].rearrange("p b k -> p (b k)"),
                              start=True, stop=True)
                for b in range(B):
                    last = pe.matmul(ps[0:KV, 3, b * D:(b + 1) * D], kinT[:, b, :], weight(f"v{a}"),
                                     start=True, stop=True)
                last.then_inc(s_kv, 1)

            def stack_k(a):
                pe.wait_ge(s_ksplit, a + 1)
                n = ST // 3
                for j in range(UG):
                    for i, part in enumerate((khi, khi, klo)):
                        last = pe.matmul(ps[n * i:n * i + n, BNUM + j // 2, 256 * (j % 2):256 * (j % 2) + B * KP],
                                         ident[:, n * j:n * j + n], part[:].bitcast(F32).rearrange("p b k -> p (b k)"),
                                         start=True, stop=True)
                last.then_inc(s_krep, 1)

            def next_context(m, g):
                if g == GROUPS - 1:
                    pe.wait_ge(s_peak[0], UNITS)
                    transposed(BS, lambda k: ctxs[:, k, :], B, KV).then_inc(s_ctxT, 1)

            def next_parts(m, g):
                if g == GROUPS - 1:
                    pe.wait_ge(s_exp[0], UNITS)
                    project_kv(1)

            def next_keys(m, g):
                if g == GROUPS - 1:
                    pe.wait_ge(s_nd[0], GROUPS)
                    stack_k(1)

            steps = dict(project=project, gate=gate, turn=turn, logits=logits, ranks=ranks, next_context=next_context,
                         next_parts=next_parts, next_keys=next_keys)

            def stack_q(a, g):
                pe.wait_ge(s_qlo, GROUPS * a + g + 1)
                if a == 0 and g == 1:
                    pe.wait_ge(s_kvfree, 1)
                for j in range(UG):
                    for i, part in enumerate((qhi, qlo)):
                        last = pe.matmul(ps[0:ST, STACK_BANKS[g] + j // 2, GQ * (j % 2):GQ * (j % 2) + GQ], sel[:, i, j, :],
                                         part[:, g % 2, :], start=(i == 0), stop=(i == 1))
                last.then_inc(s_qrep, 1)

            def tokens_in(a, g):
                pe.wait_ge(s_norm, g // (GROUPS // B) + 1 if a == 0 else B + g + 1)
                if g >= 2:
                    pe.wait_ge(s_inT, GROUPS * a + g - 1)
                elif g == 1:
                    pe.wait_ge(s_krepsb, a + 1)
                transposed(tokens_bank(g), lambda k: norm[:, GT * g + k, :], GT).then_inc(s_inTp, 1)

            def project_q(a, g):
                b, at = divmod(g, GROUPS // B)
                q = inT[:, b, GQ * at:GQ * at + GQ]
                pe.wait_ge(s_inT, GROUPS * a + g + 1)
                if g >= 2:
                    pe.wait_ge(s_rope if a == 0 else s_qlo, g - 1 if a == 0 else GROUPS + g - 1)
                last = pe.matmul(ps[:, queries_bank(g), 0:GQ], weight(f"q{a}"), q, start=True, stop=True)
                if a == 0:
                    last = pe.matmul(ps[:, queries_bank(g), GQ:2 * GQ], weight("q0p"), q, start=True, stop=True)
                last.then_inc(s_q, 1)

            def query_steps(a, turn):
                for name, g in at_turn(PE_QUERIES[a], turn):
                    if name == "tokens":
                        tokens_in(a, g)
                    elif name == "queries":
                        project_q(a, g)
                    elif name == "keys":
                        stack_k(0)
                    else:
                        stack_q(a, g)

            def attention(a):
                query_steps(a, -1)
                scores(a, 0)
                query_steps(a, 0)
                maxima(a, 0)
                scores(a, 1)
                query_steps(a, 1)
                for u in range(UNITS + max(PE_STEPS[a].values())):
                    if u < UNITS:
                        shifted_scores(a, u)
                    query_steps(a, u + 2)
                    if u + 1 < UNITS:
                        maxima(a, u + 1)
                    if u + 2 < UNITS:
                        scores(a, u + 2)
                    if AHEAD <= u < UNITS + AHEAD:
                        attend(a, u - AHEAD)
                    if u >= UNITS + AHEAD:
                        warm_up(WARM_TAIL[a], 1)
                    for name, g in due(PE_STEPS[a], u):
                        steps[name](a, g)

            def experts(m):
                cap = CAP[m]
                pe.wait_ge(s_w2[m], 16)
                pe.wait_ge(s_w1lo[m], PIECES)
                pe.wait_ge(s_slot[m], GROUPS)
                if m == 0:
                    pe.wait_ge(s_most, 1)
                    pe.wait_ge(s_kvfree, 2)

                def rows_in(e):
                    pe.wait_ge(s_xe[e], 16 * (m + 1))
                    if e >= 2:
                        pe.wait_ge(s_xTsb[m], e - 1)
                    for c in range(SC):
                        n = chunk_rows(EVEN[m], c)
                        last = pe.matmul(ps[:, e % 2, c * P:c * P + n], xe[0:n, e, c, 0:D], ident[0:n, 0:n],
                                         start=True, stop=True, is_transpose=True)
                    last.then_inc(s_xT[m], 1)

                def up(e):
                    pe.wait_ge(s_xTsb[m], e + 1)
                    for f in range(FC):
                        n = FC * e + f
                        if n >= 4:
                            pe.wait_ge(s_silu[m], n - 3)
                        parts = ((w1hi, xhi), (w1hi, xlo), (w1lo, xhi))
                        for i, (w, x) in enumerate(parts):
                            last = pe.matmul(ps[:, 2 + n % 4, 0:EVEN[m]], w[:, e, f * P:(f + 1) * P],
                                             x[:, e % 2, 0:EVEN[m]], start=(i == 0), stop=(i == len(parts) - 1))
                        last.then_inc(s_up[m], 1)

                def down(e):
                    pe.wait_ge(s_silu[m], FC * (e + 1))
                    if e >= 2:
                        pe.wait_ge(s_ye[m], e - 1)
                    for c in range(SC):
                        n = chunk_rows(cap, c)
                        for f in range(FC):
                            last = pe.matmul(ps[0:n, 6 + e % 2, c * P:(c + 1) * P], hT[:, e % 2, f, c * P:c * P + n],
                                             w2[:, e, f, :], start=(f == 0), stop=(f == FC - 1))
                    last.then_inc(s_down[m], 1)

                pe.wait_ge(s_sent[m], 16 * NPAIR // P)
                warm_up(WARM_ROWS[m], 2)
                rows_in(0)
                for e in range(E + 1):
                    if e + 1 < E:
                        rows_in(e + 1)
                    if e < E:
                        up(e)
                    if e >= 1:
                        down(e - 1)

            pe.wait_ge(s_set, 3)
            pe.wait_ge(s_ctxn, 1)
            transposed(0, lambda k: ctxn[:, k, :], B, KV).then_inc(s_ctxT, 1)
            warm_up(WARM_START)
            pe.wait_ge(s_sq, 16)
            project_kv(0)
            pe.wait_ge(s_set, 11)
            pe.wait_ge(s_kones, B)
            pe.wait_ge(s_iset, 8)
            pe.wait_ge(s_rows, 64)
            attention(0)
            experts(0)
            pe.wait_ge(s_ye[0], E)
            with overflows(pe):
                for e in range(E):
                    for b in range(B):
                        n = B * e + b
                        for f in range(FC):
                            if n >= 1:
                                pe.wait_ge(s_osilu, FC * (n - 1) + f + 1)
                            for i, w in enumerate((w1hi, w1lo)):
                                last = pe.matmul(ps[:, f, :], w[:, e, f * P:(f + 1) * P].bitcast(F32), inT[:, b, :],
                                                 start=(i == 0), stop=(i == 1))
                            last.then_inc(s_oup, 1)
                        pe.wait_ge(s_osilu, FC * (n + 1))
                        if n >= 1:
                            pe.wait_ge(s_osum, n)
                        for k in range(TB):
                            for f in range(FC):
                                last = pe.matmul(ps[:, 4, k * P:(k + 1) * P], overh[:, f, k * P:(k + 1) * P],
                                                 w2[:, e, f, :], start=(f == 0), stop=(f == FC - 1))
                        last.then_inc(s_odown, 1)
            pe.wait_ge(s_got[0], 16)
            warm_up(WARM_SUM)
            attention(1)
            experts(1)


def partner(w):
    return w.reshape(D, H, 2, DH // 2)[:, :, ::-1, :].reshape(D, D)


def grouped(w):
    return w.reshape(-1, Q4, H // Q4, DH).transpose(0, 2, 1, 3).reshape(-1, D)


def kernel(x, ctx_1024, L0_xattn_Wqkv, L0_xattn_Wout, L0_xattn_b_out, L0_xattn_Wgate, L0_xattn_b_gate,
           L0_xattn_gamma, L0_xattn_beta, L0_ffn_Wg, L0_ffn_bg, L0_ffn_W1, L0_ffn_b1, L0_ffn_W2, L0_ffn_b2,
           L1_xattn_W_Q, L1_xattn_b_Q, L1_xattn_W_K, L1_xattn_b_K, L1_xattn_W_V, L1_xattn_b_V,
           L1_xattn_W_O, L1_xattn_b_O, L1_ffn_router_w, L1_ffn_w1, L1_ffn_w2):
    import concourse.bacc as bacc
    from concourse.bass_utils import run_bass_kernel_spmd

    a = {k: np.asarray(v) for k, v in locals().items() if k not in ("bacc", "run_bass_kernel_spmd")}
    wqkv = a["L0_xattn_Wqkv"]
    wq, wk, wv = wqkv[:D].T, wqkv[D:2 * D].T, wqkv[2 * D:].T
    square = [grouped(wq), grouped(partner(wq)), grouped(wk), grouped(partner(wk)), wv, a["L0_xattn_Wout"].T, a["L0_xattn_Wgate"].T,
              grouped(a["L1_xattn_W_Q"]), grouped(a["L1_xattn_W_K"]), a["L1_xattn_W_V"], a["L1_xattn_W_O"]]
    b1 = a["L0_ffn_b1"].reshape(E * FC, P).T
    cols = [a["L0_xattn_gamma"][:, None], a["L0_xattn_beta"][:, None], a["L0_xattn_b_out"][:, None],
            grouped(a["L1_xattn_b_Q"][None, :]).T, grouped(a["L1_xattn_b_K"][None, :]).T, b1]
    rows = [a["L0_xattn_b_out"], a["L0_xattn_b_gate"], a["L1_xattn_b_O"], a["L1_xattn_b_V"], a["L0_ffn_bg"],
            a["L0_ffn_b2"].reshape(-1)]

    def up(w):
        return w.transpose(1, 0, 2).reshape(P, E * FF)

    def down(w):
        return w.reshape(E, FC, P, D).transpose(2, 0, 1, 3).reshape(P, E * FC * D)

    arrays = {
        "x": a["x"], "ctx": a["ctx_1024"], "consts": constants(), "square": np.concatenate(square, axis=1),
        "cols": np.concatenate(cols, axis=1), "rows": np.concatenate(rows)[None, :],
        "wg": a["L0_ffn_Wg"], "wr": a["L1_ffn_router_w"].T,
        "w1b": up(a["L0_ffn_W1"]), "w2b": down(a["L0_ffn_W2"]),
        "w1d": up(a["L1_ffn_w1"]), "w2d": down(a["L1_ffn_w2"]),
    }
    arrays = {k: np.ascontiguousarray(v) for k, v in arrays.items()}
    nc = bacc.Bacc("TRN2", target_bir_lowering=False, num_devices=1)
    args = [nc.dram_tensor(k, v.shape, mybir.dt.from_np(v.dtype), kind="ExternalInput").ap() for k, v in arrays.items()]
    out = nc.dram_tensor("out", (B, T, D), mybir.dt.float32, kind="ExternalOutput").ap()
    two_block_kernel(nc, *args, out)
    r = run_bass_kernel_spmd(nc, [arrays], core_ids=[0])
    return r.results[0]["out"]
```
